# Optimizing a Trainium2 kernel written in Bass

```python
import numpy as np
import jax
import jax.numpy as jnp

def _softmax(x, axis=-1):
    return jax.nn.softmax(x, axis=axis)

def _gelu(x):
    return jax.nn.gelu(x, approximate=True)

def _silu(x):
    return jax.nn.silu(x)

def _sigmoid(x):
    return jax.nn.sigmoid(x)

def _layernorm(x, axis=-1, eps=1e-05):
    m = jnp.mean(x, axis=axis, keepdims=True)
    v = jnp.var(x, axis=axis, keepdims=True)
    return (x - m) / jnp.sqrt(v + eps)

def _scatter_add(tgt, idx, src, axis=0):
    return tgt.at[idx].add(src)

def _segment_sum(src, seg, n):
    return jax.ops.segment_sum(src, seg, n)
kernel_name = 'mk_seq_preln_d1_jaxref_r8_82383b'

def setup_inputs(seed: int=0):
    np.random.seed(seed)
    _w = jnp.asarray

    def _L0_attn_setup():
        import jax, jax.numpy as jnp
        import numpy as np
        B, T, C = (4, 512, 128)

        def wkv_scan(k, v, w, u):
            Bb, Tt, Cc = k.shape
            k_t = jnp.transpose(k, (1, 0, 2))
            v_t = jnp.transpose(v, (1, 0, 2))
            num0 = jnp.zeros((Bb, Cc), dtype=jnp.float32)
            den0 = jnp.zeros((Bb, Cc), dtype=jnp.float32)
            max0 = jnp.full((Bb, Cc), -1e+38, dtype=jnp.float32)

            def step(carry, kv):
                num, den, m = carry
                kk, vv = kv
                mo = jnp.maximum(m, kk + u)
                e1 = jnp.exp(m - mo)
                e2 = jnp.exp(kk + u - mo)
                out = (e1 * num + e2 * vv) / (e1 * den + e2)
                ms = jnp.maximum(m + w, kk)
                e1s = jnp.exp(m + w - ms)
                e2s = jnp.exp(kk - ms)
                return ((e1s * num + e2s * vv, e1s * den + e2s, ms), out)
            _, outs = jax.lax.scan(step, (num0, den0, max0), (k_t, v_t))
            return jnp.transpose(outs, (1, 0, 2))
        key = jax.random.key(seed)
        ks = jax.random.split(key, 10)
        x = jax.random.normal(ks[0], (B, T, C), dtype=jnp.float32)
        Wk = jax.random.normal(ks[1], (C, C), dtype=jnp.float32) * C ** (-0.5)
        Wv = jax.random.normal(ks[2], (C, C), dtype=jnp.float32) * C ** (-0.5)
        Wr = jax.random.normal(ks[3], (C, C), dtype=jnp.float32) * C ** (-0.5)
        Wo = jax.random.normal(ks[4], (C, C), dtype=jnp.float32) * C ** (-0.5)
        time_decay = jax.random.uniform(ks[5], (C,), minval=-6.0, maxval=-5.0, dtype=jnp.float32)
        time_first = jax.random.uniform(ks[6], (C,), minval=-3.0, maxval=0.0, dtype=jnp.float32)
        mix_k = jax.random.uniform(ks[7], (1, 1, C), dtype=jnp.float32)
        mix_v = jax.random.uniform(ks[8], (1, 1, C), dtype=jnp.float32)
        mix_r = jax.random.uniform(ks[9], (1, 1, C), dtype=jnp.float32)
        return {'x': x, 'Wk': Wk, 'Wv': Wv, 'Wr': Wr, 'Wo': Wo, 'time_decay': time_decay, 'time_first': time_first, 'mix_k': mix_k, 'mix_v': mix_v, 'mix_r': mix_r}
    _L0_attn_in = _L0_attn_setup()

    def _L0_ffn_setup():
        import jax, jax.numpy as jnp
        import numpy as np
        E = 8
        K = 2

        def _moe_forward(x, router_w, w1, b1, w2, b2, w3, b3):
            B, S, H = x.shape
            xf = x.reshape(-1, H)
            logits = xf @ router_w
            probs = jax.nn.softmax(logits, axis=-1)
            top_p, top_i = jax.lax.top_k(probs, K)
            combine = jnp.sum(jax.nn.one_hot(top_i, E, dtype=probs.dtype) * top_p[..., None], axis=1)
            out = jnp.zeros_like(xf)
            for e in range(E):
                h = jax.nn.silu(xf @ w1[e] + b1[e]) * (xf @ w2[e] + b2[e])
                y = h @ w3[e] + b3[e]
                out = out + combine[:, e, None] * y
            return out.reshape(B, S, H)
        key = jax.random.key(seed)
        ks = jax.random.split(key, 8)
        B, S, H, F = (4, 256, 128, 512)
        sH = 1.0 / np.sqrt(H)
        sF = 1.0 / np.sqrt(F)
        return {'x': jax.random.normal(ks[0], (B, S, H), dtype=jnp.float32), 'router_w': jax.random.normal(ks[1], (H, E), dtype=jnp.float32) * sH, 'w1': jax.random.normal(ks[2], (E, H, F), dtype=jnp.float32) * sH, 'b1': jnp.zeros((E, F), dtype=jnp.float32), 'w2': jax.random.normal(ks[3], (E, H, F), dtype=jnp.float32) * sH, 'b2': jnp.zeros((E, F), dtype=jnp.float32), 'w3': jax.random.normal(ks[4], (E, F, H), dtype=jnp.float32) * sF, 'b3': jnp.zeros((E, H), dtype=jnp.float32)}
    _L0_ffn_in = _L0_ffn_setup()
    _d = {'L0_attn_x': _L0_attn_in['x'], 'L0_attn_Wk': _L0_attn_in['Wk'], 'L0_attn_Wv': _L0_attn_in['Wv'], 'L0_attn_Wr': _L0_attn_in['Wr'], 'L0_attn_Wo': _L0_attn_in['Wo'], 'L0_attn_time_decay': _L0_attn_in['time_decay'], 'L0_attn_time_first': _L0_attn_in['time_first'], 'L0_attn_mix_k': _L0_attn_in['mix_k'], 'L0_attn_mix_v': _L0_attn_in['mix_v'], 'L0_attn_mix_r': _L0_attn_in['mix_r'], 'L0_ffn_router_w': _L0_ffn_in['router_w'], 'L0_ffn_w1': _L0_ffn_in['w1'], 'L0_ffn_b1': _L0_ffn_in['b1'], 'L0_ffn_w2': _L0_ffn_in['w2'], 'L0_ffn_b2': _L0_ffn_in['b2'], 'L0_ffn_w3': _L0_ffn_in['w3'], 'L0_ffn_b3': _L0_ffn_in['b3']}
    _x0 = _d['L0_attn_x']
    _d['L0_attn_x'] = jax.random.normal(jax.random.fold_in(jax.random.key(seed), 1), (1, 2048, 128), dtype=_x0.dtype)
    del _x0
    return _d

def reference(L0_attn_x, L0_attn_Wk, L0_attn_Wv, L0_attn_Wr, L0_attn_Wo, L0_attn_time_decay, L0_attn_time_first, L0_attn_mix_k, L0_attn_mix_v, L0_attn_mix_r, L0_ffn_router_w, L0_ffn_w1, L0_ffn_b1, L0_ffn_w2, L0_ffn_b2, L0_ffn_w3, L0_ffn_b3):

    def _L0_attn_ref(x, Wk, Wv, Wr, Wo, time_decay, time_first, mix_k, mix_v, mix_r):
        import jax, jax.numpy as jnp
        import numpy as np
        B, T, C = (4, 512, 128)

        def wkv_scan(k, v, w, u):
            Bb, Tt, Cc = k.shape
            k_t = jnp.transpose(k, (1, 0, 2))
            v_t = jnp.transpose(v, (1, 0, 2))
            num0 = jnp.zeros((Bb, Cc), dtype=jnp.float32)
            den0 = jnp.zeros((Bb, Cc), dtype=jnp.float32)
            max0 = jnp.full((Bb, Cc), -1e+38, dtype=jnp.float32)

            def step(carry, kv):
                num, den, m = carry
                kk, vv = kv
                mo = jnp.maximum(m, kk + u)
                e1 = jnp.exp(m - mo)
                e2 = jnp.exp(kk + u - mo)
                out = (e1 * num + e2 * vv) / (e1 * den + e2)
                ms = jnp.maximum(m + w, kk)
                e1s = jnp.exp(m + w - ms)
                e2s = jnp.exp(kk - ms)
                return ((e1s * num + e2s * vv, e1s * den + e2s, ms), out)
            _, outs = jax.lax.scan(step, (num0, den0, max0), (k_t, v_t))
            return jnp.transpose(outs, (1, 0, 2))
        prev_x = jnp.pad(x, ((0, 0), (1, 0), (0, 0)))[:, :-1, :]
        r_in = x * mix_r + prev_x * (1.0 - mix_r)
        k_in = x * mix_k + prev_x * (1.0 - mix_k)
        v_in = x * mix_v + prev_x * (1.0 - mix_v)
        receptance = jnp.einsum('btc,dc->btd', r_in, Wr)
        key = jnp.einsum('btc,dc->btd', k_in, Wk)
        value = jnp.einsum('btc,dc->btd', v_in, Wv)
        w = -jnp.exp(time_decay)
        u = time_first
        wkv_out = wkv_scan(key, value, w, u)
        rwkv = jax.nn.sigmoid(receptance) * wkv_out
        return jnp.einsum('btc,dc->btd', rwkv, Wo)

    def _L0_ffn_ref(x, router_w, w1, b1, w2, b2, w3, b3):
        import jax, jax.numpy as jnp
        import numpy as np
        E = 8
        K = 2

        def _moe_forward(x, router_w, w1, b1, w2, b2, w3, b3):
            B, S, H = x.shape
            xf = x.reshape(-1, H)
            logits = xf @ router_w
            probs = jax.nn.softmax(logits, axis=-1)
            top_p, top_i = jax.lax.top_k(probs, K)
            combine = jnp.sum(jax.nn.one_hot(top_i, E, dtype=probs.dtype) * top_p[..., None], axis=1)
            out = jnp.zeros_like(xf)
            for e in range(E):
                h = jax.nn.silu(xf @ w1[e] + b1[e]) * (xf @ w2[e] + b2[e])
                y = h @ w3[e] + b3[e]
                out = out + combine[:, e, None] * y
            return out.reshape(B, S, H)
        return _moe_forward(x, router_w, w1, b1, w2, b2, w3, b3)
    x = L0_attn_x
    x = x + _L0_attn_ref(_layernorm(x, axis=-1), L0_attn_Wk, L0_attn_Wv, L0_attn_Wr, L0_attn_Wo, L0_attn_time_decay, L0_attn_time_first, L0_attn_mix_k, L0_attn_mix_v, L0_attn_mix_r)
    x = x + _L0_ffn_ref(_layernorm(x, axis=-1), L0_ffn_router_w, L0_ffn_w1, L0_ffn_b1, L0_ffn_w2, L0_ffn_b2, L0_ffn_w3, L0_ffn_b3)
    return x

_drawn_inputs = setup_inputs


def setup_inputs(seed=0):
    import zlib

    import numpy as np

    out = dict(_drawn_inputs(seed))
    spreads = {'L0_ffn_b1': (0.0, 0.301), 'L0_ffn_b2': (0.0, 0.308), 'L0_ffn_b3': (0.0, 0.1)}
    factors = {'L0_attn_time_first': 8.0}
    for name, (base, spread) in spreads.items():
        noise = np.random.default_rng([zlib.crc32(name.encode()), seed]).standard_normal(out[name].shape)
        drawn = base * np.exp(spread * noise) if base else spread * noise
        out[name] = jnp.asarray(drawn.astype(out[name].dtype))
    for name, factor in factors.items():
        out[name] = (out[name] * factor).astype(out[name].dtype)
    return out
```

```python
import concourse.bass as bass
from concourse import mybir
from contextlib import ExitStack


def rwkv_time_mix_then_routed_moe(
    nc: bass.Bass,
    x_d: bass.AP,
    wkT_d: bass.AP,
    wvT_d: bass.AP,
    wrT_d: bass.AP,
    woT_d: bass.AP,
    cols_d: bass.AP,
    router_d: bass.AP,
    wexp_d: bass.AP,
    b1_d: bass.AP,
    b2_d: bass.AP,
    b3_d: bass.AP,
    out_d: bass.AP,
):
    f32, f32r, i32 = mybir.dt.float32, mybir.dt.float32r, mybir.dt.int32
    ALU = mybir.AluOpType
    ACT = mybir.ActivationFunctionType
    AXX = mybir.AxisListType.X

    P = 128
    T, C = x_d.shape
    E = router_d.shape[1]
    F = b1_d.shape[1]
    K = 2
    NT = T // P
    CT = 4
    CW = CT * P
    NC = T // CW
    NF = F // P
    WE = 3 * F
    NS = K * T // P + E - 1
    NSP = NS + NS % 2
    KN = K * NT
    EPS = 1e-5
    NEG = -1e38
    NB3 = E * C // P
    SKIP = 2 * K * T

    xn2_d = nc.dram_tensor("xn2_rows", (T, C), f32, kind="Internal").ap()
    z_d = nc.dram_tensor("expert_rows", (K * T, C), f32, kind="Internal").ap()
    bias_d = nc.dram_tensor("bias_rows", (3, 2, E * F), f32, kind="Internal").ap()

    with ExitStack() as ctx:
        def sb(name, shape, dt=f32):
            return ctx.enter_context(nc.sbuf_tensor(name, shape, dt))

        def sem(name):
            return ctx.enter_context(nc.semaphore(name))

        ident = sb("ident", [P, P])
        ones = sb("ones", [P, P])
        before = sb("before", [P, P])
        iota_f = sb("iota_f", [P, P])
        pair_id = sb("pair_id", [P, KN])
        sel_tmp = sb("sel_tmp", [P, P])
        sel = [sb(f"sel{i}", [P, P], f32r) for i in range(3)]
        cols = sb("cols", [C, 5])
        omix = sb("omix", [C, 3])
        wdec = sb("wdec", [C, 1])
        wdec_row = sb("wdec_row", [C, CW])
        wT = sb("wT", [C, 4, C])
        wcur = sb("wcur", [C, 3, C])
        wprev = sb("wprev", [C, 3, C])
        router = sb("router", [C, E])
        w_raw = sb("w_raw", [P, 2, WE])
        w_hi = sb("w_hi", [P, E * WE], f32r)
        w_lo = sb("w_lo", [P, E * WE], f32r)
        b_raw = sb("b_raw", [P, 3, E * F // P])
        b_hi = sb("b_hi", [P, 3, E * F // P], f32r)
        b_lo = sb("b_lo", [P, 3, E * F // P], f32r)
        xs = sb("xs", [P, NT, C])
        stats = sb("stats", [P, 2 * NT, 6])
        mv = sb("mv", [P, 2 * NT, 2])
        vare = sb("vare", [P, 2 * NT])
        lnv = sb("lnv", [P, 2 * NT])
        rstd0 = sb("rstd0", [P, 2 * NT])
        nwt = sb("nwt", [P, 2 * NT])
        rstd = sb("rstd", [P, 2 * NT])
        lg = sb("lg", [P, NT, E])
        gates = sb("gates", [P, K, NT])
        te_i = sb("te_i", [1, NSP], i32)
        tb_i = sb("tb_i", [1, NSP], i32)
        t3_i = sb("t3_i", [1, NSP], i32)
        gat_i = sb("gat_i", [P, NSP], i32)
        sca_i = sb("sca_i", [P, NSP], i32)
        gat_now = sb("gat_now", [P, 2], i32)
        sca_now = sb("sca_now", [P, 2], i32)

        psum = [ctx.enter_context(nc.psum_tensor(f"bank{i}", [P, 512], f32)) for i in range(8)]

        consts_ready = sem("consts_ready")
        pool_step = sem("pool_step")
        cols_in, proj_in, router_in, bias_in = sem("cols_in"), sem("proj_in"), sem("router_in"), sem("bias_in")
        x_in = [sem(f"x_in{c}") for c in range(NC)]
        wdec_exp, mix_ready, wscaled = sem("wdec_exp"), sem("mix_ready"), sem("wscaled")
        w_in = [sem("w_in0"), sem("w_in1")]
        whi_ready, wlo_ready = sem("whi_ready"), sem("wlo_ready")
        bhi_ready, blo_ready, bias_out, bias_back, bias_zero, bias_pad = (
            sem("bhi_ready"), sem("blo_ready"), sem("bias_out"), sem("bias_back"), sem("bias_zero"), sem("bias_pad"))
        stats_ready, aggr_ready, vare_ready, lnv_ready, rstd0_ready, newton, rstd_ready = (
            sem("stats_ready"), sem("aggr_ready"), sem("vare_ready"), sem("lnv_ready"),
            sem("rstd0_ready"), sem("newton"), sem("rstd_ready"))
        xn_ready, xnT_psum, xnT_ready, xnT_pad = sem("xn_ready"), sem("xnT_psum"), sem("xnT_ready"), sem("xnT_pad")
        k_psum, v_psum, r_psum = sem("k_psum"), sem("v_psum"), sem("r_psum")
        k_ready, v_ready, absr, expr, lnsig = sem("k_ready"), sem("v_ready"), sem("absr"), sem("expr"), sem("lnsig")
        logsig_ready = sem("logsig_ready")
        state_pad, m_ready, a_ready, b_ready, d_ready, dmin_ready, dmax_ready = (
            sem("state_pad"), sem("m_ready"), sem("a_ready"), sem("b_ready"), sem("d_ready"),
            sem("dmin_ready"), sem("dmax_ready"))
        ea_ready, eb_ready, e1_ready, e2_ready = sem("ea_ready"), sem("eb_ready"), sem("e1_ready"), sem("e2_ready")
        pv_ready, num_ready, den_ready, n1_ready, n2_ready, n_ready, q1_ready, q_ready = (
            sem("pv_ready"), sem("num_ready"), sem("den_ready"), sem("n1_ready"), sem("n2_ready"),
            sem("n_ready"), sem("q1_ready"), sem("q_ready"))
        lnq_ready, scale_log, scale_ready, rwkv_ready = (
            sem("lnq_ready"), sem("scale_log"), sem("scale_ready"), sem("rwkv_ready"))
        o_psum, x2_ready, xn2_ready, xn2_out = sem("o_psum"), sem("x2_ready"), sem("xn2_ready"), [sem(f"xn2_out{c}") for c in range(NC)]
        xn2T_psum, xn2T_ready, logits_psum, logits_ready = (
            sem("xn2T_psum"), sem("xn2T_ready"), sem("logits_psum"), sem("logits_ready"))
        route, exp_ready, mask_ready, rank_psum, slot_ready, onehot_lo, onehot_hi, idx_psum = (
            sem("route"), sem("exp_ready"), sem("mask_ready"), sem("rank_psum"), sem("slot_ready"),
            sem("onehot_lo"), sem("onehot_hi"), sem("idx_psum"))
        gat_ready, sca_ready, pool_passed = sem("gat_ready"), sem("sca_ready"), sem("pool_passed")
        idx_ready, offs_ready = sem("idx_ready"), sem("offs_ready")
        rows_in = [sem("rows_in0"), sem("rows_in1")]
        rowsT_psum, xh_ready, xl_ready = sem("rowsT_psum"), sem("xh_ready"), sem("xl_ready")
        h1_psum, h2_psum, silu_ready, hid_ready = sem("h1_psum"), sem("h2_psum"), sem("silu_ready"), sem("hid_ready")
        hidT_psum, hh_ready, hl_ready = sem("hidT_psum"), sem("hh_ready"), sem("hl_ready")
        y_psum, y_ready = sem("y_psum"), sem("y_ready")
        y_out = [sem("y_out0"), sem("y_out1")]
        z_in = [sem(f"z_in{c}") for c in range(NC)]
        mixed, out_ready, out_stored = sem("mixed"), sem("out_ready"), sem("out_stored")

        def sp(name, shape, dt=f32):
            return phase.enter_context(nc.sbuf_tensor(name, shape, dt))

        with ExitStack() as phase:
            xn = sp("xn", [P, 2, CT, C])
            xnT = sp("xnT", [C, 1 + T])
            kk = sp("kk", [C, 2, CW])
            vv = sp("vv", [C, 2, CW])
            logsig = sp("logsig", [C, 2, CW])
            rtmp = sp("rtmp", [C, CW])
            mst = sp("mst", [C, 1 + T])
            num = sp("num", [C, 1 + T])
            den = sp("den", [C, 1 + T])
            ea, eb, e1, e2 = (sp(n, [C, CW]) for n in ("ea", "eb", "e1", "e2"))
            pv, n1, q1, dd = (sp(n, [C, CW]) for n in ("pv", "n1", "q1", "dd"))
            rwkv = sp("rwkv", [C, CW])
            xn2 = sp("xn2", [P, 2, CT, C])
            xn2T = sp("xn2T", [C, CW])
        late = ctx.enter_context(ExitStack())
        phase = late
        bias = sp("bias", [P, E * F], f32r)
        with ExitStack() as phase:
            onehot = sp("onehot", [P, KN, P], f32r)
            hi_oh = sp("hi_oh", [P, KN, NSP])
            hi_id = sp("hi_id", [P, KN, NSP], f32r)
            pr = sp("pr", [P, NT, E])
            cand = sp("cand", [P, NT, E])
            desc = sp("desc", [P, E])
            oh = [sp(f"oh{k}", [P, NT, E]) for k in range(K)]
            mask = sp("mask", [P, E, NT])
            tot = sp("tot", [P, E, NT])
            keep = sp("keep", [P, E, NT])
            incl = sp("incl", [P, E, NT])
            pos = sp("pos", [P, E, NT])
            tcount = sp("tcount", [P, E, NT])
            ntile = sp("ntile", [P, E])
            tend = sp("tend", [P, E])
            tbase = sp("tbase", [P, E])
            red = sp("red", [P, NT])
            slot = sp("slot", [P, KN])
            slot_i = sp("slot_i", [P, KN], i32)
            lo_i = sp("lo_i", [P, KN], i32)
            hi_i = sp("hi_i", [P, KN], i32)
            lo_f = sp("lo_f", [P, KN])
            hi_f = sp("hi_f", [P, KN])
            te_c = sp("te_c", [1, NSP, E - 1])
            te_f = sp("te_f", [1, 4, NSP])
            idx_f = sp("idx_f", [P, NSP])
            idx_z = sp("idx_z", [P, NSP])
            idx_t = sp("idx_t", [P, NSP], i32)
        with ExitStack() as phase:
            rows = sp("rows", [P, 2, C])
            xh = sp("xh", [C, 2, P], f32r)
            xl = sp("xl", [C, 2, P], f32r)
            silu = sp("silu", [P, 2, F])
            hid = sp("hid", [P, 2, F])
            hh = sp("hh", [P, 2, F], f32r)
            hl = sp("hl", [P, 2, F], f32r)
            yrow = sp("yrow", [P, 2, C])
            zrow = sp("zrow", [P, K, NT, C])

        block = ctx.enter_context(nc.Block())

        ps_T, ps_K, ps_V, ps_R, ps_O, ps_T2, ps_L, ps_X = psum
        pe_rows, pe_y = psum[0], psum[7]
        pe_h1, pe_h2, pe_hT = psum[1:3], psum[3:5], psum[5:7]

        def tiles(buf, c):
            return buf[:, c * CT:(c + 1) * CT]

        @block.sync
        def _(sp):
            sp.dma_start(cols[:], cols_d).then_inc(cols_in, 16)
            for c in range(NC):
                sp.dma_start(tiles(xs, c), x_d.rearrange("(n p) c -> p n c", p=P)[:, c * CT:(c + 1) * CT])\
                  .then_inc(x_in[c], 16)
                if c == 0:
                    for i, w in enumerate((wkT_d, wvT_d, wrT_d, woT_d)):
                        sp.dma_start(wT[:, i], w).then_inc(proj_in, 16)
            sp.dma_start(router[:], router_d).then_inc(router_in, 16)
            sp.dma_start(b_raw[:, 0], b1_d.rearrange("e (q f) -> (e q) f", q=P // E)).then_inc(bias_in, 16)
            sp.dma_start(b_raw[:, 1], b2_d.rearrange("e (q f) -> (e q) f", q=P // E)).then_inc(bias_in, 16)
            sp.dma_start(b_raw[:, 2, 0:NB3], b3_d.rearrange("e (q h) -> (e q) h", q=P // E))\
              .then_inc(bias_in, 16)
            for e in range(E):
                if e >= 2:
                    sp.wait_ge(wlo_ready, e - 1)
                sp.dma_start(w_raw[:, e % 2], wexp_d[:, e]).then_inc(w_in[e % 2], 16)
                if e == 1:
                    sp.wait_ge(bhi_ready, 1)
                    sp.wait_ge(blo_ready, 1)
                    for h, b in enumerate((b_hi, b_lo)):
                        part = b[:].bitcast(f32)
                        sp.dma_start(bias_d[0:2, h].rearrange("b (p f) -> p b f", p=P), part[:, 0:2]).then_inc(bias_out, 16)
                        sp.dma_start(bias_d[2, h, 0:E * C].rearrange("(p f) -> p f", p=P), part[:, 2, 0:NB3])\
                          .then_inc(bias_out, 16)
                        sp.dma_start(bias_d[2, h, E * C:].rearrange("(p f) -> p f", p=P), part[:, 2, NB3:])\
                          .then_inc(bias_out, 16)
            for c in range(NC):
                sp.wait_ge(xn2_ready, CT * (c + 1))
                sp.dma_start(xn2_d.rearrange("(n p) c -> p n c", p=P)[:, c * CT:(c + 1) * CT], xn2[:, c % 2])\
                  .then_inc(xn2_out[c], 16)
            sp.wait_ge(bias_out, 96)
            sp.wait_ge(bias_zero, 1)
            sp.dma_start(bias[0:6, :].bitcast(f32), bias_d.rearrange("b h f -> (b h) f"))\
              .then_inc(bias_back, 16)
            sp.wait_ge(y_out[0], 16 * ((NS + 1) // 2))
            sp.wait_ge(y_out[1], 16 * (NS // 2))
            for c in range(NC):
                for k in range(K):
                    sp.dma_start(zrow[:, k, c * CT:(c + 1) * CT],
                                 z_d[k * T + c * CW:k * T + (c + 1) * CW].rearrange("(n p) c -> p n c", p=P))\
                      .then_inc(z_in[c], 16)
            for c in range(NC):
                sp.wait_ge(out_ready, c + 1)
                sp.dma_start(out_d.rearrange("(n p) c -> p n c", p=P)[:, c * CT:(c + 1) * CT], tiles(xs, c))\
                  .then_inc(out_stored, 16)
            sp.wait_ge(out_stored, 16 * NC)

        @block.gpsimd
        def _(pool):
            g = nc.gpsimd
            g.memset(ident[:], 0.0).then_inc(pool_step, 1)
            g.memset(ones[:], 1.0).then_inc(pool_step, 1)
            pool.wait_ge(pool_step, 2)
            g.affine_select(out=ident[:], in_=ident[:], compare_op=ALU.not_equal, fill=1.0, base=0,
                            pattern=[[-1, P]], channel_multiplier=1).then_inc(pool_step, 1)
            g.affine_select(out=before[:], in_=ones[:], compare_op=ALU.is_gt, fill=0.0, base=0,
                            pattern=[[1, P]], channel_multiplier=-1).then_inc(pool_step, 1)
            g.iota(iota_f[:], pattern=[[1, P]], base=0, channel_multiplier=0,
                   allow_small_or_imprecise_dtypes=True).then_inc(pool_step, 1)
            g.iota(pair_id[:], pattern=[[P, KN]], base=1, channel_multiplier=1,
                   allow_small_or_imprecise_dtypes=True).then_inc(pool_step, 1)
            pool.wait_ge(pool_step, 6)
            g.memset(xnT[:, 0:1], 0.0).then_inc(xnT_pad, 1)
            g.memset(mst[:, 0:1], NEG).then_inc(state_pad, 1)
            g.memset(num[:, 0:1], 0.0).then_inc(state_pad, 1)
            g.memset(den[:, 0:1], 0.0).then_inc(state_pad, 1)
            n = 6
            for i in range(3):
                g.affine_select(out=sel_tmp[:], in_=ones[:], compare_op=ALU.is_ge, fill=0.0, base=-2 * i,
                                pattern=[[0, P]], channel_multiplier=1).then_inc(pool_step, 1)
                n += 1
                pool.wait_ge(pool_step, n)
                g.affine_select(out=sel[i][:], in_=sel_tmp[:], compare_op=ALU.is_ge, fill=0.0, base=2 * i + 1,
                                pattern=[[0, P]], channel_multiplier=-1).then_inc(pool_step, 1)
                n += 1
                pool.wait_ge(pool_step, n)
            g.engine_nop().then_inc(consts_ready, 1)
            pool.wait_ge(bhi_ready, 1)
            g.tensor_tensor(b_lo[:], b_raw[:], b_hi[:].bitcast(f32), ALU.subtract).then_inc(blo_ready, 1)

            for i in range(NC + 2):
                c = i
                if c < NC:
                    pool.wait_ge(rstd_ready, 1 + 2 * max(c - 2, 0) + min(c, 2))
                    if c >= 2:
                        pool.wait_ge(xnT_psum, c - 1)
                    for t in range(c * CT, (c + 1) * CT):
                        g.tensor_scalar(xn[:, c % 2, t % CT], xs[:, t], mv[:, t, 0:1], rstd[:, t:t + 1],
                                        ALU.subtract, ALU.mult).then_inc(xn_ready, 1)
                c = i - 1
                if 0 <= c < NC:
                    t0 = c * CW
                    pool.wait_ge(m_ready, c + 1)
                    pool.wait_ge(k_ready, c + 1)
                    if c:
                        pool.wait_ge(den_ready, c)
                    g.tensor_tensor(eb[:], kk[:, c % 2], mst[:, 1 + t0:1 + t0 + CW], ALU.subtract)\
                     .then_inc(b_ready, 1)
                    for e in range(2 * c, 2 * c + 2):
                        pool.wait_ge(whi_ready, e + 1)
                        g.tensor_tensor(w_lo[:, e * WE:(e + 1) * WE], w_raw[:, e % 2],
                                        w_hi[:, e * WE:(e + 1) * WE].bitcast(f32), ALU.subtract)\
                         .then_inc(wlo_ready, 1)

            pool.wait_ge(rwkv_ready, NC)
            g.memset(bias[:].bitcast(f32), 0.0).then_inc(bias_zero, 1)

            def gather(j, p, waits=True):
                if waits:
                    pool.wait_ge(rowsT_psum, j - 1)
                    pool.sem_inc(pool_passed, 1)
                g.tensor_copy(gat_now[:, p:p + 1], gat_i[:, bass.ds(j, 1)]).then_inc(gat_ready, 1)
                pool.wait_ge(gat_ready, j + 1)
                pool.sem_inc(pool_passed, 1)
                g.indirect_dma_start(
                    out=rows[:, p], out_offset=None, in_=xn2_d,
                    in_offset=bass.IndirectOffsetOnAxis(ap=gat_now[:, p:p + 1], axis=0))\
                 .then_inc(rows_in[p], 16)

            def scatter(j, p):
                pool.wait_ge(y_ready, j + 1)
                pool.sem_inc(pool_passed, 1)
                g.tensor_copy(sca_now[:, p:p + 1], sca_i[:, bass.ds(j, 1)]).then_inc(sca_ready, 1)
                pool.wait_ge(sca_ready, j + 1)
                pool.sem_inc(pool_passed, 1)
                g.indirect_dma_start(
                    out=z_d, out_offset=bass.IndirectOffsetOnAxis(ap=sca_now[:, p:p + 1], axis=0),
                    in_=yrow[:, p], in_offset=None, bounds_check=K * T - 1, oob_is_err=False)\
                 .then_inc(y_out[p], 16)

            pool.wait_ge(idx_ready, 4)
            for c in range(NC):
                pool.wait_ge(xn2_out[c], 16)
            LAG = 5
            for j in range(LAG):
                gather(j, j % 2, waits=j >= 2)
            assert (NS - LAG) % 2 == 0
            with pool.Fori(0, (NS - LAG) // 2) as jj:
                for s in range(2):
                    gather(2 * jj + (LAG + s), (LAG + s) % 2)
                    scatter(2 * jj + s, s)
            for j in range(NS - LAG, NS):
                scatter(j, j % 2)

        @block.scalar
        def _(act):
            a = nc.scalar
            act.preload_act_table_set("natural_log_exp_and_others")
            act.wait_ge(cols_in, 16)
            a.activation(wdec[:], cols[:, 0:1], ACT.Exp).then_inc(wdec_exp, 1)
            act.wait_ge(bias_in, 48)
            act.wait_ge(bias_pad, 1)
            a.activation(b_hi[:], b_raw[:], ACT.Copy).then_inc(bhi_ready, 1)

            def inverse_root_guess(c, n):
                act.wait_ge(vare_ready, n)
                a.activation(lnv[:, c * CT:(c + 1) * CT], vare[:, c * CT:(c + 1) * CT], ACT.Ln)\
                 .then_inc(lnv_ready, 1)
                act.wait_ge(lnv_ready, n)
                a.activation(rstd0[:, c * CT:(c + 1) * CT], lnv[:, c * CT:(c + 1) * CT], ACT.Exp, scale=-0.5)\
                 .then_inc(rstd0_ready, 1)

            n_ln = 0
            for i in range(NC + 2):
                c = i
                if c < NC:
                    n_ln += 1
                    inverse_root_guess(c, n_ln)
                    act.wait_ge(xnT_psum, c + 1)
                    a.activation(xnT[:, 1 + c * CW:1 + (c + 1) * CW], ps_T[:], ACT.Copy).then_inc(xnT_ready, 1)
                    act.wait_ge(k_psum, c + 1)
                    if c >= 2:
                        act.wait_ge(rwkv_ready, c - 1)
                    a.activation(kk[:, c % 2], ps_K[:], ACT.Copy).then_inc(k_ready, 1)
                    act.wait_ge(v_psum, c + 1)
                    a.activation(vv[:, c % 2], ps_V[:], ACT.Copy).then_inc(v_ready, 1)
                    act.wait_ge(r_psum, c + 1)
                    if c:
                        act.wait_ge(logsig_ready, c)
                    a.activation(rtmp[:], ps_R[:], ACT.Abs).then_inc(absr, 1)
                    act.wait_ge(absr, c + 1)
                    a.activation(rtmp[:], rtmp[:], ACT.Exp, scale=-1.0).then_inc(expr, 1)
                    act.wait_ge(expr, c + 1)
                    act.wait_ge(consts_ready, 1)
                    a.activation(rtmp[:], rtmp[:], ACT.Ln, bias=ones[:, 0:1]).then_inc(lnsig, 1)
                c = i - 1
                if 0 <= c < NC:
                    act.wait_ge(a_ready, c + 1)
                    a.activation(ea[:], ea[:], ACT.Exp).then_inc(ea_ready, 1)
                    act.wait_ge(b_ready, c + 1)
                    a.activation(eb[:], eb[:], ACT.Exp).then_inc(eb_ready, 1)
                    act.wait_ge(dmin_ready, c + 1)
                    a.activation(e2[:], e2[:], ACT.Exp).then_inc(e2_ready, 1)
                    act.wait_ge(dmax_ready, c + 1)
                    a.activation(e1[:], e1[:], ACT.Exp, scale=-1.0).then_inc(e1_ready, 1)
                    for e in range(2 * c, 2 * c + 2):
                        act.wait_ge(w_in[e % 2], 16 * (e // 2 + 1))
                        a.activation(w_hi[:, e * WE:(e + 1) * WE], w_raw[:, e % 2], ACT.Copy)\
                         .then_inc(whi_ready, 1)
                    act.wait_ge(q_ready, c + 1)
                    a.activation(q1[:], q1[:], ACT.Ln).then_inc(lnq_ready, 1)
                    act.wait_ge(scale_log, c + 1)
                    a.activation(q1[:], q1[:], ACT.Exp, scale=-1.0).then_inc(scale_ready, 1)
                c = i - 2
                if 0 <= c:
                    n_ln += 1
                    inverse_root_guess(NC + c, n_ln)
                    act.wait_ge(xn2T_psum, c + 1)
                    if c:
                        act.wait_ge(logits_psum, c)
                    a.activation(xn2T[:], ps_T2[:], ACT.Copy).then_inc(xn2T_ready, 1)
            act.wait_ge(route, 2)
            a.activation(pr[:], pr[:], ACT.Exp).then_inc(exp_ready, 1)
            act.preload_act_table_set("silu_and_others")

            def x_hi(j, p, first=False):
                act.wait_ge(rowsT_psum, j + 1)
                if not first:
                    act.wait_ge(h2_psum, j - 1)
                a.activation(xh[:, p], pe_rows[:, 0:P], ACT.Copy).then_inc(xh_ready, 1)

            def silu_of(j, p, first=False):
                act.wait_ge(h1_psum, j + 1)
                if not first:
                    act.wait_ge(hid_ready, j - 1)
                a.activation(silu[:, p], pe_h1[p][:], ACT.Silu).then_inc(silu_ready, 1)

            def hid_hi(j, p, first=False):
                act.wait_ge(hidT_psum, j + 1)
                if not first:
                    act.wait_ge(y_psum, j - 1)
                a.activation(hh[:, p], pe_hT[p][:], ACT.Copy).then_inc(hh_ready, 1)

            x_hi(0, 0, first=True)
            x_hi(1, 1, first=True)
            silu_of(0, 0, first=True)
            x_hi(2, 0)
            silu_of(1, 1, first=True)
            hid_hi(0, 0, first=True)
            x_hi(3, 1)
            silu_of(2, 0)
            hid_hi(1, 1, first=True)
            with act.Fori(0, (NS - 5) // 2) as jj:
                for s in range(2):
                    x_hi(2 * jj + (4 + s), s)
                    silu_of(2 * jj + (3 + s), (3 + s) % 2)
                    hid_hi(2 * jj + (2 + s), s)
            x_hi(NS - 1, (NS - 1) % 2)
            silu_of(NS - 2, (NS - 2) % 2)
            hid_hi(NS - 3, (NS - 3) % 2)
            silu_of(NS - 1, (NS - 1) % 2)
            hid_hi(NS - 2, (NS - 2) % 2)
            hid_hi(NS - 1, (NS - 1) % 2)

        @block.vector
        def _(dve):
            v = nc.vector
            counts = {}

            def root(c, n):
                s = slice(c * CT, (c + 1) * CT)
                for t in range(c * CT, (c + 1) * CT):
                    v.bn_stats(stats[:, t], xs[:, t % NT]).then_inc(stats_ready, 1)
                dve.wait_ge(stats_ready, CT * n)
                for t in range(c * CT, (c + 1) * CT):
                    v.bn_aggr(mv[:, t], stats[:, t]).then_inc(aggr_ready, 1)
                dve.wait_ge(aggr_ready, CT * n)
                v.tensor_scalar(vare[:, s], mv[:, s, 1], EPS, None, ALU.add).then_inc(vare_ready, 1)
                dve.wait_ge(rstd0_ready, n)
                v.tensor_tensor(nwt[:, s], rstd0[:, s], rstd0[:, s], ALU.mult).then_inc(newton, 1)
                dve.wait_ge(newton, 3 * n - 2)
                v.tensor_tensor(nwt[:, s], nwt[:, s], vare[:, s], ALU.mult).then_inc(newton, 1)
                dve.wait_ge(newton, 3 * n - 1)
                v.tensor_scalar(nwt[:, s], nwt[:, s], -0.5, 1.5, ALU.mult, ALU.add).then_inc(newton, 1)
                dve.wait_ge(newton, 3 * n)
                v.tensor_tensor(rstd[:, s], rstd0[:, s], nwt[:, s], ALU.mult).then_inc(rstd_ready, 1)

            dve.wait_ge(cols_in, 16)
            v.tensor_scalar(omix[:], cols[:, 2:5], -1.0, 1.0, ALU.mult, ALU.add).then_inc(mix_ready, 1)
            dve.wait_ge(wdec_exp, 1)
            v.tensor_scalar(wdec[:], wdec[:], -1.0, None, ALU.mult).then_inc(mix_ready, 1)
            v.memset(wdec_row[:], 0.0).then_inc(mix_ready, 1)
            dve.wait_ge(mix_ready, 3)
            v.tensor_scalar(wdec_row[:], wdec_row[:], wdec[:, 0:1], None, ALU.add).then_inc(mix_ready, 1)
            dve.wait_ge(proj_in, 64)
            for i in range(3):
                v.tensor_scalar(wcur[:, i], wT[:, i], cols[:, 2 + i:3 + i], None, ALU.mult).then_inc(wscaled, 1)
                v.tensor_scalar(wprev[:, i], wT[:, i], omix[:, i:i + 1], None, ALU.mult).then_inc(wscaled, 1)
            v.memset(b_raw[:, 2, NB3:], 0.0).then_inc(bias_pad, 1)

            n_ln = 0
            for i in range(NC + 2):
                c = i
                if c < NC:
                    dve.wait_ge(x_in[c], 16)
                    n_ln += 1
                    root(c, n_ln)
                    dve.wait_ge(lnsig, c + 1)
                    if c >= 2:
                        dve.wait_ge(scale_log, c - 1)
                    v.scalar_tensor_tensor(logsig[:, c % 2], ps_R[:], 0.0, rtmp[:], ALU.min, ALU.subtract)\
                     .then_inc(logsig_ready, 1)
                c = i - 1
                if 0 <= c < NC:
                    t0 = c * CW
                    now, prev = slice(1 + t0, 1 + t0 + CW), slice(t0, t0 + CW)
                    k_c, v_c = kk[:, c % 2], vv[:, c % 2]
                    if c == 0:
                        dve.wait_ge(state_pad, 3)
                        dve.wait_ge(mix_ready, 4)
                    dve.wait_ge(k_ready, c + 1)
                    v.tensor_tensor_scan(mst[:, now], wdec_row[:], k_c, mst[:, t0:t0 + 1], ALU.add, ALU.max)\
                     .then_inc(m_ready, 1)
                    dve.wait_ge(m_ready, c + 1)
                    v.scalar_tensor_tensor(ea[:], mst[:, prev], wdec[:, 0:1], mst[:, now], ALU.add, ALU.subtract)\
                     .then_inc(a_ready, 1)
                    v.scalar_tensor_tensor(dd[:], k_c, cols[:, 1:2], mst[:, prev], ALU.add, ALU.subtract)\
                     .then_inc(d_ready, 1)
                    dve.wait_ge(d_ready, c + 1)
                    v.tensor_scalar(e2[:], dd[:], 0.0, None, ALU.min).then_inc(dmin_ready, 1)
                    v.tensor_scalar(e1[:], dd[:], 0.0, None, ALU.max).then_inc(dmax_ready, 1)
                    dve.wait_ge(eb_ready, c + 1)
                    dve.wait_ge(v_ready, c + 1)
                    v.tensor_tensor(pv[:], eb[:], v_c, ALU.mult).then_inc(pv_ready, 1)
                    dve.wait_ge(ea_ready, c + 1)
                    v.tensor_tensor_scan(den[:, now], ea[:], eb[:], den[:, t0:t0 + 1], ALU.mult, ALU.add)\
                     .then_inc(den_ready, 1)
                    dve.wait_ge(pv_ready, c + 1)
                    v.tensor_tensor_scan(num[:, now], ea[:], pv[:], num[:, t0:t0 + 1], ALU.mult, ALU.add)\
                     .then_inc(num_ready, 1)
                    dve.wait_ge(e1_ready, c + 1)
                    dve.wait_ge(den_ready, c + 1)
                    v.tensor_tensor(q1[:], e1[:], den[:, prev], ALU.mult).then_inc(q1_ready, 1)
                    dve.wait_ge(e2_ready, c + 1)
                    v.tensor_tensor(dd[:], e2[:], v_c, ALU.mult).then_inc(n2_ready, 1)
                    dve.wait_ge(q1_ready, c + 1)
                    v.tensor_tensor(q1[:], q1[:], e2[:], ALU.add).then_inc(q_ready, 1)
                    dve.wait_ge(num_ready, c + 1)
                    v.tensor_tensor(n1[:], e1[:], num[:, prev], ALU.mult).then_inc(n1_ready, 1)
                    dve.wait_ge(n2_ready, c + 1)
                    dve.wait_ge(n1_ready, c + 1)
                    v.tensor_tensor(n1[:], n1[:], dd[:], ALU.add).then_inc(n_ready, 1)
                    dve.wait_ge(lnq_ready, c + 1)
                    dve.wait_ge(logsig_ready, c + 1)
                    v.tensor_tensor(q1[:], q1[:], logsig[:, c % 2], ALU.subtract).then_inc(scale_log, 1)
                    dve.wait_ge(scale_ready, c + 1)
                    dve.wait_ge(n_ready, c + 1)
                    if c:
                        dve.wait_ge(o_psum, c)
                    v.tensor_tensor(rwkv[:], n1[:], q1[:], ALU.mult).then_inc(rwkv_ready, 1)
                c = i - 2
                if 0 <= c:
                    dve.wait_ge(o_psum, c + 1)
                    v.tensor_tensor(tiles(xs, c), ps_O[:].rearrange("p (t c) -> p t c", c=C), tiles(xs, c), ALU.add)\
                     .then_inc(x2_ready, 1)
                    dve.wait_ge(x2_ready, c + 1)
                    n_ln += 1
                    root(NC + c, n_ln)
                    dve.wait_ge(rstd_ready, n_ln)
                    if c >= 2:
                        dve.wait_ge(xn2_out[c - 2], 16)
                        dve.wait_ge(xn2T_psum, c - 1)
                    for t in range(c * CT, (c + 1) * CT):
                        v.tensor_scalar(xn2[:, c % 2, t % CT], xs[:, t], mv[:, NT + t, 0:1],
                                        rstd[:, NT + t:NT + t + 1], ALU.subtract, ALU.mult).then_inc(xn2_ready, 1)
                    dve.wait_ge(logits_psum, c + 1)
                    v.tensor_copy(lg[:, c * CT:(c + 1) * CT],
                                  ps_L[:, c * CT * E:(c + 1) * CT * E].rearrange("p (t e) -> p t e", e=E))\
                     .then_inc(logits_ready, 1)

            n = [0]

            def step(ins):
                n[0] += 1
                ins.then_inc(route, 1)
                dve.wait_ge(route, n[0])

            def over_e(t):
                return t.unsqueeze(2).broadcast_to([P, NT, E])

            dve.wait_ge(logits_ready, NC)
            step(v.tensor_reduce(red[:], lg[:], AXX, ALU.max))
            step(v.tensor_tensor(pr[:], lg[:], over_e(red[:]), ALU.subtract))
            v.memset(keep[:], 1.0).then_inc(route, 1)
            n[0] += 1
            step(v.tensor_scalar(desc[:], iota_f[:, 0:E], -1.0, float(E), ALU.mult, ALU.add))
            step(v.memset(keep[:, :, 0:1], 0.0))
            dve.wait_ge(exp_ready, 1)
            step(v.tensor_reduce(red[:], pr[:], AXX, ALU.add))
            step(v.reciprocal(red[:], red[:]))
            step(v.tensor_tensor(pr[:], pr[:], over_e(red[:]), ALU.mult))
            for k in range(K):
                step(v.tensor_reduce(gates[:, k], pr[:], AXX, ALU.max))
                step(v.tensor_tensor(cand[:], pr[:], over_e(gates[:, k]), ALU.is_equal))
                step(v.tensor_tensor(cand[:], cand[:], desc[:].unsqueeze(1).broadcast_to([P, NT, E]), ALU.mult))
                step(v.tensor_reduce(red[:], cand[:], AXX, ALU.max))
                step(v.tensor_tensor(oh[k][:], cand[:], over_e(red[:]), ALU.is_equal))
                if k == 0:
                    step(v.scalar_tensor_tensor(pr[:], oh[0][:], -2.0, pr[:], ALU.mult, ALU.add))
            v.tensor_tensor(mask[:], oh[0][:].rearrange("p n e -> p e n"), oh[1][:].rearrange("p n e -> p e n"),
                            ALU.add).then_inc(mask_ready, 1)
            dve.wait_ge(rank_psum, 1)
            flat = "p e n -> p (e n)"
            step(v.tensor_copy(tot[:].rearrange(flat), ps_X[:, 0:E * NT]))
            step(v.tensor_tensor_scan(incl[:].rearrange(flat), keep[:].rearrange(flat), tot[:].rearrange(flat),
                                      0.0, ALU.mult, ALU.add))
            step(v.tensor_tensor(pos[:], incl[:], tot[:], ALU.subtract))
            step(v.tensor_tensor(pos[:].rearrange(flat), ps_T2[:, 0:E * NT], pos[:].rearrange(flat), ALU.add))
            step(v.tensor_scalar(tcount[:], iota_f[:, 0:NT].unsqueeze(1).broadcast_to([P, E, NT]), float(P), None,
                                 ALU.mult))
            step(v.tensor_tensor(tcount[:], incl[:, :, NT - 1:NT].broadcast_to([P, E, NT]), tcount[:], ALU.is_gt))
            step(v.tensor_reduce(ntile[:], tcount[:], AXX, ALU.add))
            step(v.tensor_tensor_scan(tend[:], ones[:, 0:E], ntile[:], 0.0, ALU.mult, ALU.add))
            step(v.tensor_tensor(tbase[:], tend[:], ntile[:], ALU.subtract))
            step(v.scalar_tensor_tensor(pos[:], tbase[:].unsqueeze(2).broadcast_to([P, E, NT]), float(P), pos[:],
                                        ALU.mult, ALU.add))
            for k in range(K):
                step(v.tensor_tensor(cand[:], oh[k][:], pos[:].rearrange("p e n -> p n e"), ALU.mult))
                step(v.tensor_reduce(slot[:, k * NT:(k + 1) * NT], cand[:], AXX, ALU.add))
            step(v.tensor_copy(slot_i[:], slot[:]))
            step(v.tensor_scalar(lo_i[:], slot_i[:], P - 1, None, ALU.bitwise_and))
            step(v.tensor_scalar(hi_i[:], slot_i[:], P.bit_length() - 1, None, ALU.logical_shift_right))
            step(v.tensor_copy(lo_f[:], lo_i[:]))
            step(v.tensor_copy(hi_f[:], hi_i[:]))
            step(v.tensor_tensor(hi_oh[:], iota_f[:, 0:NSP].unsqueeze(1).broadcast_to([P, KN, NSP]),
                                 hi_f[:].unsqueeze(2).broadcast_to([P, KN, NSP]), ALU.is_equal))
            v.tensor_tensor(hi_id[:], hi_oh[:], pair_id[:].unsqueeze(2).broadcast_to([P, KN, NSP]), ALU.mult)\
             .then_inc(onehot_hi, 1)
            for k in range(4):
                s = slice(k * KN // 4, (k + 1) * KN // 4)
                v.tensor_tensor(onehot[:, s], iota_f[:].unsqueeze(1).broadcast_to([P, KN // 4, P]),
                                lo_f[:, s].unsqueeze(2).broadcast_to([P, KN // 4, P]), ALU.is_equal)\
                 .then_inc(onehot_lo, 1)
            step(v.tensor_tensor(te_c[:], iota_f[0:1, 0:NSP].unsqueeze(2).broadcast_to([1, NSP, E - 1]),
                                 tend[0:1, 0:E - 1].unsqueeze(1).broadcast_to([1, NSP, E - 1]), ALU.is_ge))
            step(v.tensor_reduce(te_f[:, 0], te_c[:], AXX, ALU.add))
            for q, (buf, width) in enumerate(((te_i, WE), (tb_i, F), (t3_i, C))):
                step(v.tensor_scalar(te_f[:, 1 + q], te_f[:, 0], float(width), None, ALU.mult))
                v.tensor_copy(buf[:], te_f[:, 1 + q]).then_inc(offs_ready, 1)
            dve.wait_ge(idx_psum, 1)
            step(v.tensor_scalar(idx_f[:], ps_L[:, 256:256 + NSP], -1.0, None, ALU.add))
            step(v.tensor_scalar(idx_z[:], idx_f[:], 0.0, float(SKIP), ALU.is_lt, ALU.mult))
            step(v.tensor_tensor(idx_z[:], idx_z[:], idx_f[:], ALU.add))
            v.tensor_copy(sca_i[:], idx_z[:]).then_inc(idx_ready, 1)
            step(v.tensor_copy(idx_t[:], idx_f[:]))
            v.tensor_scalar(gat_i[:], idx_t[:], T - 1, None, ALU.bitwise_and).then_inc(idx_ready, 3)

            def x_lo(j, p):
                dve.wait_ge(xh_ready, j + 1)
                v.tensor_tensor(xl[:, p], pe_rows[:, 0:P], xh[:, p].bitcast(f32), ALU.subtract)\
                 .then_inc(xl_ready, 1)

            def hidden(j, p, first=False):
                dve.wait_ge(silu_ready, j + 1)
                dve.wait_ge(h2_psum, j + 1)
                if not first:
                    dve.wait_ge(hidT_psum, j - 1)
                v.tensor_tensor(hid[:, p], silu[:, p], pe_h2[p][:], ALU.mult).then_inc(hid_ready, 1)

            def hid_lo(j, p):
                dve.wait_ge(hh_ready, j + 1)
                v.tensor_tensor(hl[:, p], pe_hT[p][:], hh[:, p].bitcast(f32), ALU.subtract).then_inc(hl_ready, 1)

            def y_copy(j, p, scattered=None):
                dve.wait_ge(y_psum, j + 1)
                if scattered is not None:
                    dve.wait_ge(y_out[p], scattered)
                v.tensor_copy(yrow[:, p], pe_y[:, 0:C]).then_inc(y_ready, 1)

            x_lo(0, 0)
            x_lo(1, 1)
            hidden(0, 0, first=True)
            x_lo(2, 0)
            hidden(1, 1, first=True)
            hid_lo(0, 0)
            x_lo(3, 1)
            hidden(2, 0)
            hid_lo(1, 1)
            y_copy(0, 0)
            x_lo(4, 0)
            hidden(3, 1)
            hid_lo(2, 0)
            y_copy(1, 1)
            with dve.Fori(0, (NS - 7) // 2) as jj:
                for s in range(2):
                    x_lo(2 * jj + (5 + s), (5 + s) % 2)
                    hidden(2 * jj + (4 + s), s)
                    hid_lo(2 * jj + (3 + s), (3 + s) % 2)
                    y_copy(2 * jj + (2 + s), s, scattered=16 * jj + 16)
            for j in range(NS - 3, NS + 2):
                if j + 1 < NS:
                    x_lo(j + 1, (j + 1) % 2)
                if j < NS:
                    hidden(j, j % 2)
                if j - 1 < NS:
                    hid_lo(j - 1, (j - 1) % 2)
                y_copy(j - 2, j % 2, scattered=16 * ((j - 2) // 2))

            for c in range(NC):
                dve.wait_ge(z_in[c], 16 * K)
                for k in range(K):
                    for t in range(c * CT, (c + 1) * CT):
                        last = v.scalar_tensor_tensor(xs[:, t], zrow[:, k, t], gates[:, k, t:t + 1], xs[:, t],
                                                      ALU.mult, ALU.add)
                        last.then_inc(mixed, 1)
                    if k == 0:
                        dve.wait_ge(mixed, 2 * CT * c + CT)
                dve.wait_ge(mixed, 2 * CT * (c + 1))
                v.sem_inc(out_ready, 1)

        @block.tensor
        def _(pe):
            m = nc.tensor
            pe.wait_ge(consts_ready, 1)
            for i in range(NC + 2):
                c = i
                if c < NC:
                    pe.wait_ge(xn_ready, CT * (c + 1))
                    if c:
                        pe.wait_ge(xnT_ready, c)
                    for t in range(CT):
                        last = m.transpose(ps_T[:, t * P:(t + 1) * P], xn[:, c % 2, t], ident[:])
                    last.then_inc(xnT_psum, 1)
                    pe.wait_ge(xnT_ready, c + 1)
                    if c == 0:
                        pe.wait_ge(wscaled, 6)
                        pe.wait_ge(xnT_pad, 1)
                    for w, (bank, done, free) in enumerate(((ps_K, k_psum, k_ready), (ps_V, v_psum, v_ready),
                                                            (ps_R, r_psum, logsig_ready))):
                        if c:
                            pe.wait_ge(free, c)
                        m.matmul(bank[:], wcur[:, w], xnT[:, 1 + c * CW:1 + (c + 1) * CW], start=True, stop=False)
                        m.matmul(bank[:], wprev[:, w], xnT[:, c * CW:(c + 1) * CW], start=False, stop=True)\
                         .then_inc(done, 1)
                c = i - 2
                if 0 <= c:
                    pe.wait_ge(rwkv_ready, c + 1)
                    if c:
                        pe.wait_ge(x2_ready, c)
                    for t in range(CT):
                        last = m.matmul(ps_O[:, t * C:(t + 1) * C], rwkv[:, t * P:(t + 1) * P], wT[:, 3],
                                        start=True, stop=True)
                    last.then_inc(o_psum, 1)
                    pe.wait_ge(xn2_ready, CT * (c + 1))
                    if c:
                        pe.wait_ge(xn2T_ready, c)
                    for t in range(CT):
                        last = m.transpose(ps_T2[:, t * P:(t + 1) * P], xn2[:, c % 2, t], ident[:])
                    last.then_inc(xn2T_psum, 1)
                    pe.wait_ge(xn2T_ready, c + 1)
                    if c == 0:
                        pe.wait_ge(router_in, 16)
                    else:
                        pe.wait_ge(logits_ready, c)
                    for t in range(CT):
                        n = (c * CT + t) * E
                        last = m.matmul(ps_L[:, n:n + E], xn2T[:, t * P:(t + 1) * P], router[:], start=True, stop=True)
                    last.then_inc(logits_psum, 1)
            pe.wait_ge(mask_ready, 1)
            m.matmul(ps_X[:, 0:E * NT], ones[:], mask[:].rearrange("p e n -> p (e n)"), start=True, stop=True)
            m.matmul(ps_T2[:, 0:E * NT], before[:], mask[:].rearrange("p e n -> p (e n)"), start=True, stop=True)\
             .then_inc(rank_psum, 1)
            pe.wait_ge(onehot_hi, 1)
            for kn in range(KN):
                if kn % (KN // 4) == 0:
                    pe.wait_ge(onehot_lo, kn // (KN // 4) + 1)
                last = m.matmul(ps_L[:, 256:256 + NSP], onehot[:, kn], hi_id[:, kn], start=kn == 0, stop=kn == KN - 1)
            last.then_inc(idx_psum, 1)

            def rows_T(j, p, landed, first=False):
                pe.wait_ge(rows_in[p], landed)
                if not first:
                    pe.wait_ge(xl_ready, j)
                m.transpose(pe_rows[:, 0:P], rows[:, p], ident[:]).then_inc(rowsT_psum, 1)

            def up(j, p, first=False):
                e = pe.value_load(te_i[0:1, bass.ds(j, 1)], min_val=0, max_val=(E - 1) * WE)
                b = pe.value_load(tb_i[0:1, bass.ds(j, 1)], min_val=0, max_val=(E - 1) * F)
                pe.wait_ge(xl_ready, j + 1)
                for h, (bank, done, free) in enumerate(((pe_h1, h1_psum, silu_ready), (pe_h2, h2_psum, hid_ready))):
                    if not first:
                        pe.wait_ge(free, j - 1)
                    m.matmul(bank[p][:], sel[h][:], bias[:, bass.ds(b, F)], start=True, stop=False)
                    m.matmul(bank[p][:], xh[:, p], w_hi[:, bass.ds(e + h * F, F)], start=False, stop=False)
                    m.matmul(bank[p][:], xh[:, p], w_lo[:, bass.ds(e + h * F, F)], start=False, stop=False)
                    m.matmul(bank[p][:], xl[:, p], w_hi[:, bass.ds(e + h * F, F)], start=False, stop=True)\
                     .then_inc(done, 1)

            def hid_T(j, p, first=False):
                pe.wait_ge(hid_ready, j + 1)
                if not first:
                    pe.wait_ge(hl_ready, j - 1)
                for f in range(NF):
                    last = m.transpose(pe_hT[p][:, f * P:(f + 1) * P], hid[:, p, f * P:(f + 1) * P], ident[:])
                last.then_inc(hidT_psum, 1)

            def down(j, p, first=False):
                e = pe.value_load(te_i[0:1, bass.ds(j, 1)], min_val=0, max_val=(E - 1) * WE)
                b = pe.value_load(t3_i[0:1, bass.ds(j, 1)], min_val=0, max_val=(E - 1) * C)
                pe.wait_ge(hl_ready, j + 1)
                if not first:
                    pe.wait_ge(y_ready, j)
                m.matmul(pe_y[:, 0:C], sel[2][:], bias[:, bass.ds(b, C)], start=True, stop=False)
                for f in range(NF):
                    part = slice(f * P, (f + 1) * P)
                    at = e + (2 * F + f * C)
                    m.matmul(pe_y[:, 0:C], hh[:, p, part], w_hi[:, bass.ds(at, C)], start=False, stop=False)
                    m.matmul(pe_y[:, 0:C], hh[:, p, part], w_lo[:, bass.ds(at, C)], start=False, stop=False)
                    last = m.matmul(pe_y[:, 0:C], hl[:, p, part], w_hi[:, bass.ds(at, C)], start=False,
                                    stop=f == NF - 1)
                last.then_inc(y_psum, 1)

            pe.wait_ge(offs_ready, 3)
            pe.wait_ge(whi_ready, E)
            pe.wait_ge(wlo_ready, E)
            pe.wait_ge(bias_back, 16)
            rows_T(0, 0, 16, first=True)
            rows_T(1, 1, 16)
            up(0, 0, first=True)
            rows_T(2, 0, 32)
            up(1, 1, first=True)
            hid_T(0, 0, first=True)
            rows_T(3, 1, 32)
            up(2, 0)
            hid_T(1, 1, first=True)
            down(0, 0, first=True)
            rows_T(4, 0, 48)
            up(3, 1)
            hid_T(2, 0)
            down(1, 1)
            with pe.Fori(0, (NS - 5) // 2) as jj:
                for s in range(2):
                    rows_T(2 * jj + (5 + s), (5 + s) % 2, 16 * jj + 48 + 16 * s)
                    up(2 * jj + (4 + s), s)
                    hid_T(2 * jj + (3 + s), (3 + s) % 2)
                    down(2 * jj + (2 + s), s)
            up(NS - 1, (NS - 1) % 2)
            hid_T(NS - 2, (NS - 2) % 2)
            down(NS - 3, (NS - 3) % 2)
            hid_T(NS - 1, (NS - 1) % 2)
            down(NS - 2, (NS - 2) % 2)
            down(NS - 1, (NS - 1) % 2)


def kernel(**inputs):
    import numpy as np
    import concourse.bacc as bacc
    from concourse.bass_utils import run_bass_kernel_spmd

    a = {k: np.asarray(v) for k, v in inputs.items()}
    B, T, C = a["L0_attn_x"].shape
    E, H, F = a["L0_ffn_w1"].shape
    P = 128
    w3 = a["L0_ffn_w3"].reshape(E, F // P, P, H).transpose(2, 0, 1, 3).reshape(P, E, F // P * H)
    laid = {
        "x": a["L0_attn_x"].reshape(T, C),
        "wkT": a["L0_attn_Wk"].T,
        "wvT": a["L0_attn_Wv"].T,
        "wrT": a["L0_attn_Wr"].T,
        "woT": a["L0_attn_Wo"].T,
        "cols": np.stack([a["L0_attn_time_decay"], a["L0_attn_time_first"], a["L0_attn_mix_k"].reshape(C),
                          a["L0_attn_mix_v"].reshape(C), a["L0_attn_mix_r"].reshape(C)], axis=1),
        "router": a["L0_ffn_router_w"],
        "wexp": np.concatenate([a["L0_ffn_w1"].transpose(1, 0, 2), a["L0_ffn_w2"].transpose(1, 0, 2), w3], axis=2),
        "b1": a["L0_ffn_b1"],
        "b2": a["L0_ffn_b2"],
        "b3": a["L0_ffn_b3"],
    }
    nc = bacc.Bacc("TRN2", target_bir_lowering=False, num_devices=1)
    arrays, args = {}, []
    for name, v in laid.items():
        v = np.ascontiguousarray(v)
        arrays[f"in_{name}"] = v
        args.append(nc.dram_tensor(f"in_{name}", v.shape, mybir.dt.from_np(v.dtype), kind="ExternalInput").ap())
    args.append(nc.dram_tensor("out_0", (T, C), mybir.dt.float32, kind="ExternalOutput").ap())
    rwkv_time_mix_then_routed_moe(nc, *args)
    r = run_bass_kernel_spmd(nc, [arrays], core_ids=[0])
    return r.results[0]["out_0"].reshape(B, T, C)
```

```python
import concourse.bass as bass
from concourse import mybir
from contextlib import ExitStack


def rwkv_time_mix_then_routed_moe(
    nc: bass.Bass,
    x_d: bass.AP,
    wkT_d: bass.AP,
    wvT_d: bass.AP,
    wrT_d: bass.AP,
    woT_d: bass.AP,
    cols_d: bass.AP,
    router_d: bass.AP,
    wexp_d: bass.AP,
    b1_d: bass.AP,
    b2_d: bass.AP,
    b3_d: bass.AP,
    out_d: bass.AP,
):
    f32, f32r, i32 = mybir.dt.float32, mybir.dt.float32r, mybir.dt.int32
    ALU = mybir.AluOpType
    ACT = mybir.ActivationFunctionType
    AXX = mybir.AxisListType.X

    P = 128
    T, C = x_d.shape
    E = router_d.shape[1]
    F = b1_d.shape[1]
    K = 2
    NT = T // P
    CT = 4
    CW = CT * P
    NC = T // CW
    NF = F // P
    WE = 3 * F
    NS = K * T // P + E - 1
    NSP = NS + NS % 2
    KN = K * NT
    EPS = 1e-5
    NEG = -1e38
    NB3 = E * C // P
    SKIP = 2 * K * T

    xn2_d = nc.dram_tensor("xn2_rows", (T, C), f32, kind="Internal").ap()
    z_d = nc.dram_tensor("expert_rows", (K * T, C), f32, kind="Internal").ap()
    bias_d = nc.dram_tensor("bias_rows", (3, 2, E * F), f32, kind="Internal").ap()

    with ExitStack() as ctx:
        def sb(name, shape, dt=f32):
            return ctx.enter_context(nc.sbuf_tensor(name, shape, dt))

        def sem(name):
            return ctx.enter_context(nc.semaphore(name))

        ident = sb("ident", [P, P])
        ones = sb("ones", [P, P])
        before = sb("before", [P, P])
        iota_f = sb("iota_f", [P, P])
        pair_id = sb("pair_id", [P, KN])
        sel_tmp = sb("sel_tmp", [P, P])
        sel = [sb(f"sel{i}", [P, P], f32r) for i in range(3)]
        cols = sb("cols", [C, 5])
        omix = sb("omix", [C, 3])
        wdec = sb("wdec", [C, 1])
        wdec_row = sb("wdec_row", [C, CW])
        wT = sb("wT", [C, 4, C])
        wcur = sb("wcur", [C, 3, C])
        wprev = sb("wprev", [C, 3, C])
        router = sb("router", [C, E])
        w_raw = sb("w_raw", [P, 2, WE])
        w_two = sb("w_two", [P, E * 2 * WE], f32r)
        b_raw = sb("b_raw", [P, 3, E * F // P])
        b_hi = sb("b_hi", [P, 3, E * F // P], f32r)
        b_lo = sb("b_lo", [P, 3, E * F // P], f32r)
        xs = sb("xs", [P, NT, C])
        stats = sb("stats", [P, 2 * NT, 6])
        mv = sb("mv", [P, 2 * NT, 2])
        vare = sb("vare", [P, 2 * NT])
        lnv = sb("lnv", [P, 2 * NT])
        rstd0 = sb("rstd0", [P, 2 * NT])
        nwt = sb("nwt", [P, 2 * NT])
        rstd = sb("rstd", [P, 2 * NT])
        nmr = sb("nmr", [P, 2 * NT])
        gates = sb("gates", [P, K, NT])
        te_i = sb("te_i", [1, NSP], i32)
        gat_i = sb("gat_i", [P, NSP], i32)
        sca_i = sb("sca_i", [P, NSP], i32)
        gat_now = sb("gat_now", [P, 2], i32)
        sca_now = sb("sca_now", [P, 2], i32)

        psum = [ctx.enter_context(nc.psum_tensor(f"bank{i}", [P, 512], f32)) for i in range(8)]

        consts_ready = sem("consts_ready")
        pool_step = sem("pool_step")
        cols_in, proj_in, router_in, bias_in = sem("cols_in"), sem("proj_in"), sem("router_in"), sem("bias_in")
        x_in = [sem(f"x_in{c}") for c in range(NC)]
        wdec_exp, mix_ready, wscaled = sem("wdec_exp"), sem("mix_ready"), sem("wscaled")
        w_in = [sem("w_in0"), sem("w_in1")]
        whi_ready, wlo_ready = sem("whi_ready"), sem("wlo_ready")
        bhi_ready, blo_ready, bias_out, bias_back, bias_zero, bias_pad = (
            sem("bhi_ready"), sem("blo_ready"), sem("bias_out"), sem("bias_back"), sem("bias_zero"), sem("bias_pad"))
        stats_ready, aggr_ready, vare_ready, lnv_ready, rstd0_ready, newton, rstd_ready = (
            sem("stats_ready"), sem("aggr_ready"), sem("vare_ready"), sem("lnv_ready"),
            sem("rstd0_ready"), sem("newton"), sem("rstd_ready"))
        nmr_ready, qsum_ready = sem("nmr_ready"), sem("qsum_ready")
        xn_ready, xnT_psum, xnT_ready, xnT_pad = sem("xn_ready"), sem("xnT_psum"), sem("xnT_ready"), sem("xnT_pad")
        k_psum, v_psum, r_psum = sem("k_psum"), sem("v_psum"), sem("r_psum")
        k_ready, v_ready, absr, er_ready = sem("k_ready"), sem("v_ready"), sem("absr"), sem("er_ready")
        state_pad, m_ready, a_ready, b_ready, d_ready, dmin_ready, dmax_ready = (
            sem("state_pad"), sem("m_ready"), sem("a_ready"), sem("b_ready"), sem("d_ready"),
            sem("dmin_ready"), sem("dmax_ready"))
        ea_ready, eb_ready, e1_ready, e2_ready = sem("ea_ready"), sem("eb_ready"), sem("e1_ready"), sem("e2_ready")
        pv_ready, num_ready, den_ready, n1_ready, n2_ready, n_ready, q1_ready, q_ready = (
            sem("pv_ready"), sem("num_ready"), sem("den_ready"), sem("n1_ready"), sem("n2_ready"),
            sem("n_ready"), sem("q1_ready"), sem("q_ready"))
        lnq_ready, scale_log, scale_ready, rwkv_ready = (
            sem("lnq_ready"), sem("scale_log"), sem("scale_ready"), sem("rwkv_ready"))
        o_psum, x2_ready, xn2_ready, xn2_out = sem("o_psum"), sem("x2_ready"), sem("xn2_ready"), [sem(f"xn2_out{c}") for c in range(NC)]
        xn2T_psum, xn2T_ready, logits_psum = sem("xn2T_psum"), sem("xn2T_ready"), sem("logits_psum")
        route, exp_ready, mask_ready, rank_psum, slot_ready, onehot_lo, onehot_hi, idx_psum = (
            sem("route"), sem("exp_ready"), sem("mask_ready"), sem("rank_psum"), sem("slot_ready"),
            sem("onehot_lo"), sem("onehot_hi"), sem("idx_psum"))
        gat_ready, sca_ready, pool_passed = sem("gat_ready"), sem("sca_ready"), sem("pool_passed")
        idx_ready, offs_ready = sem("idx_ready"), sem("offs_ready")
        rows_in = [sem("rows_in0"), sem("rows_in1")]
        rowsT_psum, xh_ready, xl_ready = sem("rowsT_psum"), sem("xh_ready"), sem("xl_ready")
        h1_psum, h2_psum, silu_ready, hid_ready = sem("h1_psum"), sem("h2_psum"), sem("silu_ready"), sem("hid_ready")
        hidT_psum, hh_ready, hl_ready = sem("hidT_psum"), sem("hh_ready"), sem("hl_ready")
        y_psum, y_ready = sem("y_psum"), sem("y_ready")
        y_out = [sem("y_out0"), sem("y_out1")]
        z_in = [sem(f"z_in{c}") for c in range(NC)]
        mixed, out_ready, out_stored = sem("mixed"), sem("out_ready"), sem("out_stored")

        def sp(name, shape, dt=f32):
            return phase.enter_context(nc.sbuf_tensor(name, shape, dt))

        with ExitStack() as phase:
            xn = sp("xn", [P, 2, CT, C])
            xnT = sp("xnT", [C, 1 + T])
            kk = sp("kk", [C, 2, CW])
            vv = sp("vv", [C, 2, CW])
            er = sp("er", [C, 2, CW])
            mst = sp("mst", [C, 1 + T])
            num = sp("num", [C, 1 + T])
            den = sp("den", [C, 1 + T])
            ea, eb, e1, e2 = (sp(n, [C, CW]) for n in ("ea", "eb", "e1", "e2"))
            pv, n1, n2, q1, dd = (sp(n, [C, CW]) for n in ("pv", "n1", "n2", "q1", "dd"))
            rwkv = sp("rwkv", [C, CW])
            xn2 = sp("xn2", [P, 2, CT, C])
            xn2T = sp("xn2T", [C, CW])
        late = ctx.enter_context(ExitStack())
        phase = late
        bias = sp("bias", [P, E * F], f32r)
        with ExitStack() as phase:
            onehot = sp("onehot", [P, KN, P], f32r)
            hi_oh = sp("hi_oh", [P, KN, NSP])
            hi_id = sp("hi_id", [P, KN, NSP], f32r)
            pr = sp("pr", [P, NT, E])
            cand = sp("cand", [P, NT, E])
            desc = sp("desc", [P, E])
            oh = [sp(f"oh{k}", [P, NT, E]) for k in range(K)]
            mask = sp("mask", [P, E, NT])
            tot = sp("tot", [P, E, NT])
            keep = sp("keep", [P, E, NT])
            incl = sp("incl", [P, E, NT])
            pos = sp("pos", [P, E, NT])
            tcount = sp("tcount", [P, E, NT])
            ntile = sp("ntile", [P, E])
            tend = sp("tend", [P, E])
            tbase = sp("tbase", [P, E])
            red = sp("red", [P, NT])
            slot = sp("slot", [P, KN])
            slot_i = sp("slot_i", [P, KN], i32)
            lo_i = sp("lo_i", [P, KN], i32)
            hi_i = sp("hi_i", [P, KN], i32)
            lo_f = sp("lo_f", [P, KN])
            hi_f = sp("hi_f", [P, KN])
            te_c = sp("te_c", [1, NSP, E - 1])
            te_f = sp("te_f", [1, 1, NSP])
            idx_f = sp("idx_f", [P, NSP])
            idx_z = sp("idx_z", [P, NSP])
            idx_t = sp("idx_t", [P, NSP], i32)
        with ExitStack() as phase:
            rows = sp("rows", [P, 2, C])
            xh = sp("xh", [C, 2, P], f32r)
            xl = sp("xl", [C, 2, P], f32r)
            silu = sp("silu", [P, 2, F])
            hid = sp("hid", [P, 2, F])
            hh = sp("hh", [P, 2, F], f32r)
            hl = sp("hl", [P, 2, F], f32r)
            yrow = sp("yrow", [P, 2, C])
            zrow = sp("zrow", [P, K, NT, C])

        block = ctx.enter_context(nc.Block())

        ps_T, ps_K, ps_V, ps_O, ps_T2, ps_L = psum[0:6]
        ps_R = psum[6:8]
        pe_rows, pe_y = psum[0], psum[7]
        pe_h1, pe_h2, pe_hT = psum[1:3], psum[3:5], psum[5:7]

        def tiles(buf, c):
            return buf[:, c * CT:(c + 1) * CT]

        def ln_tiles(g):
            if g < 2:
                return slice(CT, NT) if g else slice(0, CT)
            return slice(NT + (g - 2) * CT, NT + (g - 1) * CT)

        def ln_count(g):
            return ln_tiles(g).stop

        def raw_blocks(e):
            raw = w_raw[:, e % 2]
            return (raw[:, 0:2 * F].rearrange("p (b f) -> p b f", f=F),
                    raw[:, 2 * F:].rearrange("p (b c) -> p b c", c=C))

        def split_blocks(e):
            at = e * 2 * WE
            up = w_two[:, at:at + 4 * F].rearrange("p (b h f) -> p h b f", h=2, f=F)
            down = w_two[:, at + 4 * F:at + 2 * WE].rearrange("p (b h c) -> p h b c", h=2, c=C)
            return (up[:, 0], up[:, 1]), (down[:, 0], down[:, 1])

        @block.sync
        def _(sp):
            sp.dma_start(cols[:], cols_d).then_inc(cols_in, 16)
            for c in range(NC):
                sp.dma_start(tiles(xs, c), x_d.rearrange("(n p) c -> p n c", p=P)[:, c * CT:(c + 1) * CT])\
                  .then_inc(x_in[c], 16)
                if c == 0:
                    for i, w in enumerate((wkT_d, wvT_d, wrT_d, woT_d)):
                        sp.dma_start(wT[:, i], w).then_inc(proj_in, 16)
            sp.dma_start(router[:], router_d).then_inc(router_in, 16)
            sp.dma_start(b_raw[:, 0], b1_d.rearrange("e (q f) -> (e q) f", q=P // E)).then_inc(bias_in, 16)
            sp.dma_start(b_raw[:, 1], b2_d.rearrange("e (q f) -> (e q) f", q=P // E)).then_inc(bias_in, 16)
            sp.dma_start(b_raw[:, 2, 0:NB3], b3_d.rearrange("e (q h) -> (e q) h", q=P // E))\
              .then_inc(bias_in, 16)
            def load_weights(e):
                if e >= 2:
                    sp.wait_ge(wlo_ready, e - 1)
                sp.dma_start(w_raw[:, e % 2], wexp_d[:, e]).then_inc(w_in[e % 2], 16)

            load_weights(0)
            load_weights(1)
            sp.wait_ge(bhi_ready, 1)
            sp.wait_ge(blo_ready, 1)
            for h, b in enumerate((b_hi, b_lo)):
                part = b[:].bitcast(f32)
                sp.dma_start(bias_d[0:2, h].rearrange("b (p f) -> p b f", p=P), part[:, 0:2]).then_inc(bias_out, 16)
                sp.dma_start(bias_d[2, h, 0:E * C].rearrange("(p f) -> p f", p=P), part[:, 2, 0:NB3])\
                  .then_inc(bias_out, 16)
                sp.dma_start(bias_d[2, h, E * C:].rearrange("(p f) -> p f", p=P), part[:, 2, NB3:])\
                  .then_inc(bias_out, 16)
            for c in range(NC):
                load_weights(2 + c)
                sp.wait_ge(xn2_ready, c + 1)
                sp.dma_start(xn2_d.rearrange("(n p) c -> p n c", p=P)[:, c * CT:(c + 1) * CT], xn2[:, c % 2])\
                  .then_inc(xn2_out[c], 16)
            for e in range(2 + NC, E):
                load_weights(e)
            sp.wait_ge(bias_out, 96)
            sp.wait_ge(bias_zero, 1)
            sp.dma_start(bias[0:6, :].bitcast(f32), bias_d.rearrange("b h f -> (b h) f"))\
              .then_inc(bias_back, 16)
            sp.wait_ge(y_out[0], 16 * ((NS + 1) // 2))
            sp.wait_ge(y_out[1], 16 * (NS // 2))
            for c in range(NC):
                for k in range(K):
                    sp.dma_start(zrow[:, k, c * CT:(c + 1) * CT],
                                 z_d[k * T + c * CW:k * T + (c + 1) * CW].rearrange("(n p) c -> p n c", p=P))\
                      .then_inc(z_in[c], 16)
            for c in range(NC):
                sp.wait_ge(out_ready, c + 1)
                sp.dma_start(out_d.rearrange("(n p) c -> p n c", p=P)[:, c * CT:(c + 1) * CT], tiles(xs, c))\
                  .then_inc(out_stored, 16)
            sp.wait_ge(out_stored, 16 * NC)

        @block.gpsimd
        def _(pool):
            g = nc.gpsimd
            g.memset(ident[:], 0.0).then_inc(pool_step, 1)
            g.memset(ones[:], 1.0).then_inc(pool_step, 1)
            pool.wait_ge(pool_step, 2)
            g.affine_select(out=ident[:], in_=ident[:], compare_op=ALU.not_equal, fill=1.0, base=0,
                            pattern=[[-1, P]], channel_multiplier=1).then_inc(pool_step, 1)
            g.affine_select(out=before[:], in_=ones[:], compare_op=ALU.is_gt, fill=0.0, base=0,
                            pattern=[[1, P]], channel_multiplier=-1).then_inc(pool_step, 1)
            g.iota(iota_f[:], pattern=[[1, P]], base=0, channel_multiplier=0,
                   allow_small_or_imprecise_dtypes=True).then_inc(pool_step, 1)
            g.iota(pair_id[:], pattern=[[P, KN]], base=1, channel_multiplier=1,
                   allow_small_or_imprecise_dtypes=True).then_inc(pool_step, 1)
            pool.wait_ge(pool_step, 6)
            g.memset(xnT[:, 0:1], 0.0).then_inc(xnT_pad, 1)
            g.memset(mst[:, 0:1], NEG).then_inc(state_pad, 1)
            g.memset(num[:, 0:1], 0.0).then_inc(state_pad, 1)
            g.memset(den[:, 0:1], 0.0).then_inc(state_pad, 1)
            n = 6
            for i in range(3):
                g.affine_select(out=sel_tmp[:], in_=ones[:], compare_op=ALU.is_ge, fill=0.0, base=-2 * i,
                                pattern=[[0, P]], channel_multiplier=1).then_inc(pool_step, 1)
                n += 1
                pool.wait_ge(pool_step, n)
                g.affine_select(out=sel[i][:], in_=sel_tmp[:], compare_op=ALU.is_ge, fill=0.0, base=2 * i + 1,
                                pattern=[[0, P]], channel_multiplier=-1).then_inc(pool_step, 1)
                n += 1
                pool.wait_ge(pool_step, n)
            g.engine_nop().then_inc(consts_ready, 1)
            pool.wait_ge(bhi_ready, 1)
            g.tensor_tensor(b_lo[:], b_raw[:], b_hi[:].bitcast(f32), ALU.subtract).then_inc(blo_ready, 1)

            def weights_lo(e):
                pool.wait_ge(whi_ready, e + 1)
                for whole, (hi, lo) in zip(raw_blocks(e), split_blocks(e)):
                    last = g.tensor_tensor(lo, whole, hi.bitcast(f32), ALU.subtract)
                last.then_inc(wlo_ready, 1)

            def key_exponent(c):
                pool.wait_ge(m_ready, c + 1)
                g.tensor_tensor(eb[:], kk[:, c % 2], mst[:, 1 + c * CW:1 + (c + 1) * CW], ALU.subtract)\
                 .then_inc(b_ready, 1)
                pool.wait_ge(eb_ready, c + 1)
                pool.wait_ge(v_ready, c + 1)
                g.tensor_tensor(pv[:], eb[:], vv[:, c % 2], ALU.mult).then_inc(pv_ready, 1)

            key_exponent(0)
            for c in range(NC):
                pool.wait_ge(n1_ready, c + 1)
                g.tensor_tensor(n1[:], n1[:], n2[:], ALU.add).then_inc(n_ready, 1)
                if c + 1 < NC:
                    key_exponent(c + 1)
                weights_lo(c)
            pool.wait_ge(rwkv_ready, NC)
            g.memset(bias[:].bitcast(f32), 0.0).then_inc(bias_zero, 1)

            for e in range(NC, E):
                weights_lo(e)

            def gather(j, p, waits=True):
                if waits:
                    pool.wait_ge(rowsT_psum, j - 1)
                    pool.sem_inc(pool_passed, 1)
                g.tensor_copy(gat_now[:, p:p + 1], gat_i[:, bass.ds(j, 1)]).then_inc(gat_ready, 1)
                pool.wait_ge(gat_ready, j + 1)
                pool.sem_inc(pool_passed, 1)
                g.indirect_dma_start(
                    out=rows[:, p], out_offset=None, in_=xn2_d,
                    in_offset=bass.IndirectOffsetOnAxis(ap=gat_now[:, p:p + 1], axis=0))\
                 .then_inc(rows_in[p], 16)

            def scatter(j, p):
                pool.wait_ge(y_ready, j + 1)
                pool.sem_inc(pool_passed, 1)
                g.tensor_copy(sca_now[:, p:p + 1], sca_i[:, bass.ds(j, 1)]).then_inc(sca_ready, 1)
                pool.wait_ge(sca_ready, j + 1)
                pool.sem_inc(pool_passed, 1)
                g.indirect_dma_start(
                    out=z_d, out_offset=bass.IndirectOffsetOnAxis(ap=sca_now[:, p:p + 1], axis=0),
                    in_=yrow[:, p], in_offset=None, bounds_check=K * T - 1, oob_is_err=False)\
                 .then_inc(y_out[p], 16)

            pool.wait_ge(idx_ready, 4)
            for c in range(NC):
                pool.wait_ge(xn2_out[c], 16)
            LAG = 5
            for j in range(LAG):
                gather(j, j % 2, waits=j >= 2)
            assert (NS - LAG) % 2 == 0
            with pool.Fori(0, (NS - LAG) // 2) as jj:
                for s in range(2):
                    gather(2 * jj + (LAG + s), (LAG + s) % 2)
                    scatter(2 * jj + s, s)
            for j in range(NS - LAG, NS):
                scatter(j, j % 2)

        @block.scalar
        def _(act):
            a = nc.scalar
            act.preload_act_table_set("natural_log_exp_and_others")
            act.wait_ge(cols_in, 16)
            a.activation(wdec[:], cols[:, 0:1], ACT.Exp).then_inc(wdec_exp, 1)
            act.wait_ge(bias_in, 48)
            act.wait_ge(bias_pad, 1)
            a.activation(b_hi[:], b_raw[:], ACT.Copy).then_inc(bhi_ready, 1)

            def inverse_root_guess(g):
                s, n = ln_tiles(g), g + 1
                act.wait_ge(vare_ready, n)
                a.activation(lnv[:, s], vare[:, s], ACT.Ln).then_inc(lnv_ready, 1)
                act.wait_ge(lnv_ready, n)
                a.activation(rstd0[:, s], lnv[:, s], ACT.Exp, scale=-0.5).then_inc(rstd0_ready, 1)

            def token_rows(c):
                act.wait_ge(nmr_ready, 1 + (c > 0))
                if c >= 2:
                    act.wait_ge(xnT_psum, c - 1)
                for t in range(c * CT, (c + 1) * CT):
                    last = a.activation(xn[:, c % 2, t % CT], xs[:, t], ACT.Identity, bias=nmr[:, t:t + 1],
                                        scale=rstd[:, t:t + 1])
                last.then_inc(xn_ready, 1)
                act.wait_ge(xnT_psum, c + 1)
                a.activation(xnT[:, 1 + c * CW:1 + (c + 1) * CW], ps_T[:], ACT.Copy).then_inc(xnT_ready, 1)

            def projections(c):
                act.wait_ge(k_psum, c + 1)
                if c >= 2:
                    act.wait_ge(rwkv_ready, c - 1)
                a.activation(kk[:, c % 2], ps_K[:], ACT.Copy).then_inc(k_ready, 1)
                act.wait_ge(v_psum, c + 1)
                a.activation(vv[:, c % 2], ps_V[:], ACT.Copy).then_inc(v_ready, 1)
                act.wait_ge(r_psum, c + 1)
                a.activation(er[:, c % 2], ps_R[c % 2][:], ACT.Abs).then_inc(absr, 1)
                act.wait_ge(absr, c + 1)
                a.activation(er[:, c % 2], er[:, c % 2], ACT.Exp, scale=-1.0).then_inc(er_ready, 1)

            def weights_hi(e):
                act.wait_ge(w_in[e % 2], 16 * (e // 2 + 1))
                for whole, (hi, _) in zip(raw_blocks(e), split_blocks(e)):
                    last = a.activation(hi, whole, ACT.Copy)
                last.then_inc(whi_ready, 1)

            def exponentials(c, part):
                if part == 0:
                    act.wait_ge(dmin_ready, c + 1)
                    a.activation(e2[:], e2[:], ACT.Exp).then_inc(e2_ready, 1)
                else:
                    act.wait_ge(dmax_ready, c + 1)
                    a.activation(e1[:], e1[:], ACT.Exp, scale=-1.0).then_inc(e1_ready, 1)
                    act.wait_ge(b_ready, c + 1)
                    a.activation(eb[:], eb[:], ACT.Exp).then_inc(eb_ready, 1)

            def decay_exponential(c):
                act.wait_ge(a_ready, c + 1)
                a.activation(ea[:], ea[:], ACT.Exp).then_inc(ea_ready, 1)

            inverse_root_guess(0)
            token_rows(0)
            inverse_root_guess(1)
            projections(0)
            exponentials(0, 0)
            exponentials(0, 1)
            decay_exponential(0)
            token_rows(1)
            projections(1)
            token_rows(2)
            for c in range(NC + 1):
                if c >= 1:
                    inverse_root_guess(1 + c)
                if c < NC:
                    act.wait_ge(q_ready, c + 1)
                    a.activation(q1[:], q1[:], ACT.Ln).then_inc(lnq_ready, 1)
                if c >= 1:
                    act.wait_ge(nmr_ready, 2 + c)
                    if c >= 3:
                        act.wait_ge(xn2_out[c - 3], 16)
                        act.wait_ge(xn2T_psum, c - 2)
                    for t in range((c - 1) * CT, c * CT):
                        last = a.activation(xn2[:, (c - 1) % 2, t % CT], xs[:, t], ACT.Identity,
                                            bias=nmr[:, NT + t:NT + t + 1], scale=rstd[:, NT + t:NT + t + 1])
                    last.then_inc(xn2_ready, 1)
                if c + 1 < NC:
                    exponentials(c + 1, 0)
                if c < NC:
                    act.wait_ge(scale_log, c + 1)
                    a.activation(q1[:], q1[:], ACT.Exp).then_inc(scale_ready, 1)
                if c + 1 < NC:
                    exponentials(c + 1, 1)
                    decay_exponential(c + 1)
                if c >= 1:
                    act.wait_ge(xn2T_psum, c)
                    if c >= 2:
                        act.wait_ge(logits_psum, c - 1)
                    a.activation(xn2T[:], ps_T2[:], ACT.Copy).then_inc(xn2T_ready, 1)
                if c + 2 < NC:
                    projections(c + 2)
                if c + 3 < NC:
                    token_rows(c + 3)
                if c < NC:
                    weights_hi(c)
            for e in range(NC, E - 1):
                weights_hi(e)
            act.wait_ge(route, 2)
            a.activation(pr[:], pr[:], ACT.Exp).then_inc(exp_ready, 1)
            weights_hi(E - 1)
            act.preload_act_table_set("silu_and_others")

            def x_hi(j, p, first=False):
                act.wait_ge(rowsT_psum, j + 1)
                if not first:
                    act.wait_ge(h2_psum, j - 1)
                a.activation(xh[:, p], pe_rows[:, 0:P], ACT.Copy).then_inc(xh_ready, 1)

            def silu_of(j, p, first=False):
                act.wait_ge(h1_psum, j + 1)
                if not first:
                    act.wait_ge(hid_ready, j - 1)
                a.activation(silu[:, p], pe_h1[p][:], ACT.Silu).then_inc(silu_ready, 1)

            def hid_hi(j, p, first=False):
                act.wait_ge(hidT_psum, j + 1)
                if not first:
                    act.wait_ge(y_psum, j - 1)
                a.activation(hh[:, p], pe_hT[p][:], ACT.Copy).then_inc(hh_ready, 1)

            x_hi(0, 0, first=True)
            x_hi(1, 1, first=True)
            silu_of(0, 0, first=True)
            x_hi(2, 0)
            silu_of(1, 1, first=True)
            hid_hi(0, 0, first=True)
            x_hi(3, 1)
            silu_of(2, 0)
            hid_hi(1, 1, first=True)
            with act.Fori(0, (NS - 5) // 2) as jj:
                for s in range(2):
                    x_hi(2 * jj + (4 + s), s)
                    silu_of(2 * jj + (3 + s), (3 + s) % 2)
                    hid_hi(2 * jj + (2 + s), s)
            x_hi(NS - 1, (NS - 1) % 2)
            silu_of(NS - 2, (NS - 2) % 2)
            hid_hi(NS - 3, (NS - 3) % 2)
            silu_of(NS - 1, (NS - 1) % 2)
            hid_hi(NS - 2, (NS - 2) % 2)
            hid_hi(NS - 1, (NS - 1) % 2)

        @block.vector
        def _(dve):
            v = nc.vector
            def statistics(g):
                s, n = ln_tiles(g), ln_count(g)
                for t in range(s.start, s.stop):
                    v.bn_stats(stats[:, t], xs[:, t % NT]).then_inc(stats_ready, 1)

            def variance(g):
                s, n = ln_tiles(g), ln_count(g)
                dve.wait_ge(stats_ready, n)
                for t in range(s.start, s.stop):
                    v.bn_aggr(mv[:, t], stats[:, t]).then_inc(aggr_ready, 1)
                dve.wait_ge(aggr_ready, n)
                v.tensor_scalar(vare[:, s], mv[:, s, 1], EPS, None, ALU.add).then_inc(vare_ready, 1)

            def newton_step(g):
                s, n = ln_tiles(g), g + 1
                dve.wait_ge(rstd0_ready, n)
                v.tensor_tensor(nwt[:, s], rstd0[:, s], rstd0[:, s], ALU.mult).then_inc(newton, 1)
                dve.wait_ge(newton, 3 * n - 2)
                v.tensor_tensor(nwt[:, s], nwt[:, s], vare[:, s], ALU.mult).then_inc(newton, 1)
                dve.wait_ge(newton, 3 * n - 1)
                v.tensor_scalar(nwt[:, s], nwt[:, s], -0.5, 1.5, ALU.mult, ALU.add).then_inc(newton, 1)
                dve.wait_ge(newton, 3 * n)
                v.tensor_tensor(rstd[:, s], rstd0[:, s], nwt[:, s], ALU.mult).then_inc(rstd_ready, 1)
                dve.wait_ge(rstd_ready, n)
                v.scalar_tensor_tensor(nmr[:, s], mv[:, s, 0], -1.0, rstd[:, s], ALU.mult, ALU.mult)\
                 .then_inc(nmr_ready, 1)

            dve.wait_ge(cols_in, 16)
            v.tensor_scalar(omix[:], cols[:, 2:5], -1.0, 1.0, ALU.mult, ALU.add).then_inc(mix_ready, 1)
            dve.wait_ge(wdec_exp, 1)
            v.tensor_scalar(wdec[:], wdec[:], -1.0, None, ALU.mult).then_inc(mix_ready, 1)
            v.memset(wdec_row[:], 0.0).then_inc(mix_ready, 1)
            dve.wait_ge(mix_ready, 3)
            v.tensor_scalar(wdec_row[:], wdec_row[:], wdec[:, 0:1], None, ALU.add).then_inc(mix_ready, 1)
            dve.wait_ge(proj_in, 64)
            for i in range(3):
                v.tensor_scalar(wcur[:, i], wT[:, i], cols[:, 2 + i:3 + i], None, ALU.mult).then_inc(wscaled, 1)
                v.tensor_scalar(wprev[:, i], wT[:, i], omix[:, i:i + 1], None, ALU.mult).then_inc(wscaled, 1)
            v.memset(b_raw[:, 2, NB3:], 0.0).then_inc(bias_pad, 1)

            def running_maximum(c):
                t0 = c * CW
                if c == 0:
                    dve.wait_ge(state_pad, 3)
                    dve.wait_ge(mix_ready, 4)
                dve.wait_ge(k_ready, c + 1)
                v.tensor_tensor_scan(mst[:, 1 + t0:1 + t0 + CW], wdec_row[:], kk[:, c % 2], mst[:, t0:t0 + 1],
                                     ALU.add, ALU.max).then_inc(m_ready, 1)
                dve.wait_ge(m_ready, c + 1)
                v.scalar_tensor_tensor(dd[:], kk[:, c % 2], cols[:, 1:2], mst[:, t0:t0 + CW], ALU.add, ALU.subtract)\
                 .then_inc(d_ready, 1)

            def d_min(c):
                dve.wait_ge(d_ready, c + 1)
                v.tensor_scalar(e2[:], dd[:], 0.0, None, ALU.min).then_inc(dmin_ready, 1)

            def d_max(c):
                v.tensor_scalar(e1[:], dd[:], 0.0, None, ALU.max).then_inc(dmax_ready, 1)

            def decay_exponent(c):
                t0 = c * CW
                v.scalar_tensor_tensor(ea[:], mst[:, t0:t0 + CW], wdec[:, 0:1], mst[:, 1 + t0:1 + t0 + CW],
                                       ALU.add, ALU.subtract).then_inc(a_ready, 1)

            dve.wait_ge(x_in[0], 16)
            statistics(0)
            variance(0)
            newton_step(0)
            for c in range(1, NC):
                dve.wait_ge(x_in[c], 16)
            statistics(1)
            variance(1)
            newton_step(1)
            running_maximum(0)
            d_min(0)
            d_max(0)
            decay_exponent(0)
            for c in range(NC + 1):
                t0 = c * CW
                now, prev = slice(1 + t0, 1 + t0 + CW), slice(t0, t0 + CW)
                if c < NC:
                    dve.wait_ge(e2_ready, c + 1)
                    dve.wait_ge(v_ready, c + 1)
                    v.tensor_tensor(n2[:], e2[:], vv[:, c % 2], ALU.mult).then_inc(n2_ready, 1)
                    dve.wait_ge(ea_ready, c + 1)
                    dve.wait_ge(eb_ready, c + 1)
                    v.tensor_tensor_scan(den[:, now], ea[:], eb[:], den[:, t0:t0 + 1], ALU.mult, ALU.add)\
                     .then_inc(den_ready, 1)
                    dve.wait_ge(e1_ready, c + 1)
                    dve.wait_ge(den_ready, c + 1)
                    v.tensor_tensor(q1[:], e1[:], den[:, prev], ALU.mult).then_inc(q1_ready, 1)
                if c >= 1:
                    dve.wait_ge(o_psum, c)
                    v.tensor_tensor(tiles(xs, c - 1), ps_O[:].rearrange("p (t c) -> p t c", c=C), tiles(xs, c - 1),
                                    ALU.add).then_inc(x2_ready, 1)
                if c < NC:
                    dve.wait_ge(pv_ready, c + 1)
                    v.tensor_tensor_scan(num[:, now], ea[:], pv[:], num[:, t0:t0 + 1], ALU.mult, ALU.add)\
                     .then_inc(num_ready, 1)
                if c >= 1:
                    dve.wait_ge(x2_ready, c)
                    statistics(1 + c)
                if c < NC:
                    dve.wait_ge(q1_ready, c + 1)
                    v.tensor_tensor(q1[:], e2[:], q1[:], ALU.add).then_inc(qsum_ready, 1)
                    dve.wait_ge(num_ready, c + 1)
                    v.tensor_tensor(n1[:], e1[:], num[:, prev], ALU.mult).then_inc(n1_ready, 1)
                if c >= 1:
                    variance(1 + c)
                if c < NC:
                    dve.wait_ge(er_ready, c + 1)
                    dve.wait_ge(qsum_ready, c + 1)
                    v.scalar_tensor_tensor(q1[:], er[:, c % 2], 1.0, q1[:], ALU.add, ALU.mult).then_inc(q_ready, 1)
                if c >= 1:
                    newton_step(1 + c)
                if c + 1 < NC:
                    running_maximum(c + 1)
                    d_min(c + 1)
                if c < NC:
                    dve.wait_ge(lnq_ready, c + 1)
                    v.scalar_tensor_tensor(q1[:], ps_R[c % 2][:], 0.0, q1[:], ALU.min, ALU.subtract)\
                     .then_inc(scale_log, 1)
                if c + 1 < NC:
                    d_max(c + 1)
                    decay_exponent(c + 1)
                if c < NC:
                    dve.wait_ge(scale_ready, c + 1)
                    dve.wait_ge(n_ready, c + 1)
                    if c:
                        dve.wait_ge(o_psum, c)
                    v.tensor_tensor(rwkv[:], n1[:], q1[:], ALU.mult).then_inc(rwkv_ready, 1)

            n = [0]

            def step(ins):
                n[0] += 1
                ins.then_inc(route, 1)
                dve.wait_ge(route, n[0])

            def over_e(t):
                return t.unsqueeze(2).broadcast_to([P, NT, E])

            logits = ps_L[:, 0:NT * E].rearrange("p (n e) -> p n e", e=E)
            dve.wait_ge(logits_psum, NC)
            step(v.tensor_reduce(red[:], logits, AXX, ALU.max))
            step(v.tensor_tensor(pr[:], logits, over_e(red[:]), ALU.subtract))
            v.memset(keep[:], 1.0).then_inc(route, 1)
            n[0] += 1
            step(v.tensor_scalar(desc[:], iota_f[:, 0:E], -1.0, float(E), ALU.mult, ALU.add))
            step(v.memset(keep[:, :, 0:1], 0.0))
            dve.wait_ge(exp_ready, 1)
            step(v.tensor_reduce(red[:], pr[:], AXX, ALU.add))
            step(v.reciprocal(red[:], red[:]))
            step(v.tensor_tensor(pr[:], pr[:], over_e(red[:]), ALU.mult))
            for k in range(K):
                step(v.tensor_reduce(gates[:, k], pr[:], AXX, ALU.max))
                step(v.tensor_tensor(cand[:], pr[:], over_e(gates[:, k]), ALU.is_equal))
                step(v.tensor_tensor(cand[:], cand[:], desc[:].unsqueeze(1).broadcast_to([P, NT, E]), ALU.mult))
                step(v.tensor_reduce(red[:], cand[:], AXX, ALU.max))
                step(v.tensor_tensor(oh[k][:], cand[:], over_e(red[:]), ALU.is_equal))
                if k == 0:
                    step(v.scalar_tensor_tensor(pr[:], oh[0][:], -2.0, pr[:], ALU.mult, ALU.add))
            v.tensor_tensor(mask[:], oh[0][:].rearrange("p n e -> p e n"), oh[1][:].rearrange("p n e -> p e n"),
                            ALU.add).then_inc(mask_ready, 1)
            dve.wait_ge(rank_psum, 1)
            flat = "p e n -> p (e n)"
            step(v.tensor_copy(tot[:].rearrange(flat), ps_K[:, 0:E * NT]))
            step(v.tensor_tensor_scan(incl[:].rearrange(flat), keep[:].rearrange(flat), tot[:].rearrange(flat),
                                      0.0, ALU.mult, ALU.add))
            step(v.tensor_tensor(pos[:], incl[:], tot[:], ALU.subtract))
            step(v.tensor_tensor(pos[:].rearrange(flat), ps_T2[:, 0:E * NT], pos[:].rearrange(flat), ALU.add))
            step(v.tensor_scalar(tcount[:], iota_f[:, 0:NT].unsqueeze(1).broadcast_to([P, E, NT]), float(P), None,
                                 ALU.mult))
            step(v.tensor_tensor(tcount[:], incl[:, :, NT - 1:NT].broadcast_to([P, E, NT]), tcount[:], ALU.is_gt))
            step(v.tensor_reduce(ntile[:], tcount[:], AXX, ALU.add))
            step(v.tensor_tensor_scan(tend[:], ones[:, 0:E], ntile[:], 0.0, ALU.mult, ALU.add))
            step(v.tensor_tensor(tbase[:], tend[:], ntile[:], ALU.subtract))
            step(v.scalar_tensor_tensor(pos[:], tbase[:].unsqueeze(2).broadcast_to([P, E, NT]), float(P), pos[:],
                                        ALU.mult, ALU.add))
            for k in range(K):
                step(v.tensor_tensor(cand[:], oh[k][:], pos[:].rearrange("p e n -> p n e"), ALU.mult))
                step(v.tensor_reduce(slot[:, k * NT:(k + 1) * NT], cand[:], AXX, ALU.add))
            step(v.tensor_copy(slot_i[:], slot[:]))
            step(v.tensor_scalar(lo_i[:], slot_i[:], P - 1, None, ALU.bitwise_and))
            step(v.tensor_scalar(hi_i[:], slot_i[:], P.bit_length() - 1, None, ALU.logical_shift_right))
            step(v.tensor_copy(lo_f[:], lo_i[:]))
            step(v.tensor_copy(hi_f[:], hi_i[:]))
            step(v.tensor_tensor(hi_oh[:], iota_f[:, 0:NSP].unsqueeze(1).broadcast_to([P, KN, NSP]),
                                 hi_f[:].unsqueeze(2).broadcast_to([P, KN, NSP]), ALU.is_equal))
            v.tensor_tensor(hi_id[:], hi_oh[:], pair_id[:].unsqueeze(2).broadcast_to([P, KN, NSP]), ALU.mult)\
             .then_inc(onehot_hi, 1)
            for k in range(4):
                s = slice(k * KN // 4, (k + 1) * KN // 4)
                v.tensor_tensor(onehot[:, s], iota_f[:].unsqueeze(1).broadcast_to([P, KN // 4, P]),
                                lo_f[:, s].unsqueeze(2).broadcast_to([P, KN // 4, P]), ALU.is_equal)\
                 .then_inc(onehot_lo, 1)
            step(v.tensor_tensor(te_c[:], iota_f[0:1, 0:NSP].unsqueeze(2).broadcast_to([1, NSP, E - 1]),
                                 tend[0:1, 0:E - 1].unsqueeze(1).broadcast_to([1, NSP, E - 1]), ALU.is_ge))
            step(v.tensor_reduce(te_f[:, 0], te_c[:], AXX, ALU.add))
            v.tensor_copy(te_i[:], te_f[:, 0]).then_inc(offs_ready, 1)
            dve.wait_ge(idx_psum, 1)
            step(v.tensor_scalar(idx_f[:], ps_L[:, 256:256 + NSP], -1.0, None, ALU.add))
            step(v.tensor_scalar(idx_z[:], idx_f[:], 0.0, float(SKIP), ALU.is_lt, ALU.mult))
            step(v.tensor_tensor(idx_z[:], idx_z[:], idx_f[:], ALU.add))
            v.tensor_copy(sca_i[:], idx_z[:]).then_inc(idx_ready, 1)
            step(v.tensor_copy(idx_t[:], idx_f[:]))
            v.tensor_scalar(gat_i[:], idx_t[:], T - 1, None, ALU.bitwise_and).then_inc(idx_ready, 3)

            def x_lo(j, p):
                dve.wait_ge(xh_ready, j + 1)
                v.tensor_tensor(xl[:, p], pe_rows[:, 0:P], xh[:, p].bitcast(f32), ALU.subtract)\
                 .then_inc(xl_ready, 1)

            def hidden(j, p, first=False):
                dve.wait_ge(silu_ready, j + 1)
                dve.wait_ge(h2_psum, j + 1)
                if not first:
                    dve.wait_ge(hidT_psum, j - 1)
                v.tensor_tensor(hid[:, p], silu[:, p], pe_h2[p][:], ALU.mult).then_inc(hid_ready, 1)

            def hid_lo(j, p):
                dve.wait_ge(hh_ready, j + 1)
                v.tensor_tensor(hl[:, p], pe_hT[p][:], hh[:, p].bitcast(f32), ALU.subtract).then_inc(hl_ready, 1)

            def y_copy(j, p, scattered=None):
                dve.wait_ge(y_psum, j + 1)
                if scattered is not None:
                    dve.wait_ge(y_out[p], scattered)
                v.tensor_reduce(yrow[:, p], pe_y[:, 0:2 * C].rearrange("p (h c) -> p c h", h=2), AXX, ALU.add)\
                 .then_inc(y_ready, 1)

            x_lo(0, 0)
            x_lo(1, 1)
            hidden(0, 0, first=True)
            x_lo(2, 0)
            hidden(1, 1, first=True)
            hid_lo(0, 0)
            x_lo(3, 1)
            hidden(2, 0)
            hid_lo(1, 1)
            y_copy(0, 0)
            x_lo(4, 0)
            hidden(3, 1)
            hid_lo(2, 0)
            y_copy(1, 1)
            with dve.Fori(0, (NS - 7) // 2) as jj:
                for s in range(2):
                    x_lo(2 * jj + (5 + s), (5 + s) % 2)
                    hidden(2 * jj + (4 + s), s)
                    hid_lo(2 * jj + (3 + s), (3 + s) % 2)
                    y_copy(2 * jj + (2 + s), s, scattered=16 * jj + 16)
            for j in range(NS - 3, NS + 2):
                if j + 1 < NS:
                    x_lo(j + 1, (j + 1) % 2)
                if j < NS:
                    hidden(j, j % 2)
                if j - 1 < NS:
                    hid_lo(j - 1, (j - 1) % 2)
                y_copy(j - 2, j % 2, scattered=16 * ((j - 2) // 2))

            for c in range(NC):
                dve.wait_ge(z_in[c], 16 * K)
                for k in range(K):
                    for t in range(c * CT, (c + 1) * CT):
                        last = v.scalar_tensor_tensor(xs[:, t], zrow[:, k, t], gates[:, k, t:t + 1], xs[:, t],
                                                      ALU.mult, ALU.add)
                        last.then_inc(mixed, 1)
                    if k == 0:
                        dve.wait_ge(mixed, 2 * CT * c + CT)
                dve.wait_ge(mixed, 2 * CT * (c + 1))
                v.sem_inc(out_ready, 1)

        @block.tensor
        def _(pe):
            m = nc.tensor
            pe.wait_ge(consts_ready, 1)
            def rows_to_channels(c):
                pe.wait_ge(xn_ready, c + 1)
                if c:
                    pe.wait_ge(xnT_ready, c)
                for t in range(CT):
                    last = m.transpose(ps_T[:, t * P:(t + 1) * P], xn[:, c % 2, t], ident[:])
                last.then_inc(xnT_psum, 1)

            def project(c):
                pe.wait_ge(xnT_ready, c + 1)
                if c == 0:
                    pe.wait_ge(wscaled, 6)
                    pe.wait_ge(xnT_pad, 1)
                for w, (bank, done, free, n) in enumerate(((ps_K, k_psum, k_ready, c), (ps_V, v_psum, v_ready, c),
                                                           (ps_R[c % 2], r_psum, scale_log, c - 1))):
                    if n >= 1:
                        pe.wait_ge(free, n)
                    m.matmul(bank[:], wcur[:, w], xnT[:, 1 + c * CW:1 + (c + 1) * CW], start=True, stop=False)
                    m.matmul(bank[:], wprev[:, w], xnT[:, c * CW:(c + 1) * CW], start=False, stop=True)\
                     .then_inc(done, 1)

            rows_to_channels(0)
            project(0)
            rows_to_channels(1)
            project(1)
            rows_to_channels(2)
            for c in range(NC + 1):
                if c >= 1:
                    pe.wait_ge(xn2_ready, c)
                    if c >= 2:
                        pe.wait_ge(xn2T_ready, c - 1)
                    for t in range(CT):
                        last = m.transpose(ps_T2[:, t * P:(t + 1) * P], xn2[:, (c - 1) % 2, t], ident[:])
                    last.then_inc(xn2T_psum, 1)
                if c < NC:
                    pe.wait_ge(rwkv_ready, c + 1)
                    if c:
                        pe.wait_ge(x2_ready, c)
                    for t in range(CT):
                        last = m.matmul(ps_O[:, t * C:(t + 1) * C], rwkv[:, t * P:(t + 1) * P], wT[:, 3],
                                        start=True, stop=True)
                    last.then_inc(o_psum, 1)
                if c >= 1:
                    pe.wait_ge(xn2T_ready, c)
                    if c == 1:
                        pe.wait_ge(router_in, 16)
                    for t in range(CT):
                        n = ((c - 1) * CT + t) * E
                        last = m.matmul(ps_L[:, n:n + E], xn2T[:, t * P:(t + 1) * P], router[:], start=True, stop=True)
                    last.then_inc(logits_psum, 1)
                if c + 2 < NC:
                    project(c + 2)
                if c + 3 < NC:
                    rows_to_channels(c + 3)
            pe.wait_ge(mask_ready, 1)
            m.matmul(ps_K[:, 0:E * NT], ones[:], mask[:].rearrange("p e n -> p (e n)"), start=True, stop=True)
            m.matmul(ps_T2[:, 0:E * NT], before[:], mask[:].rearrange("p e n -> p (e n)"), start=True, stop=True)\
             .then_inc(rank_psum, 1)
            pe.wait_ge(onehot_hi, 1)
            for kn in range(KN):
                if kn % (KN // 4) == 0:
                    pe.wait_ge(onehot_lo, kn // (KN // 4) + 1)
                last = m.matmul(ps_L[:, 256:256 + NSP], onehot[:, kn], hi_id[:, kn], start=kn == 0, stop=kn == KN - 1)
            last.then_inc(idx_psum, 1)

            def expert_of(j):
                _, (e,) = nc.values_load_multi_w_load_instructions(
                    te_i[0:1, bass.ds(j, 1)], engines=[mybir.EngineType.PE], min_val=0, max_val=E - 1,
                    skip_runtime_bounds_check_because="it is a count over E - 1 comparisons")
                return e

            def rows_T(j, p, landed, first=False):
                pe.wait_ge(rows_in[p], landed)
                if not first:
                    pe.wait_ge(xl_ready, j)
                m.transpose(pe_rows[:, 0:P], rows[:, p], ident[:]).then_inc(rowsT_psum, 1)

            def up(j, p, first=False):
                e = expert_of(j)
                pe.wait_ge(xl_ready, j + 1)
                for h, (bank, done, free) in enumerate(((pe_h1, h1_psum, silu_ready), (pe_h2, h2_psum, hid_ready))):
                    if not first:
                        pe.wait_ge(free, j - 1)
                    hi, lo = (w_two[:, bass.ds(e * (2 * WE) + (2 * h + i) * F, F)] for i in range(2))
                    m.matmul(bank[p][:], sel[h][:], bias[:, bass.ds(e * F, F)], start=True, stop=False)
                    m.matmul(bank[p][:], xh[:, p], hi, start=False, stop=False)
                    m.matmul(bank[p][:], xh[:, p], lo, start=False, stop=False)
                    m.matmul(bank[p][:], xl[:, p], hi, start=False, stop=True)\
                     .then_inc(done, 1)

            def hid_T(j, p, first=False):
                pe.wait_ge(hid_ready, j + 1)
                if not first:
                    pe.wait_ge(hl_ready, j - 1)
                for f in range(NF):
                    last = m.transpose(pe_hT[p][:, f * P:(f + 1) * P], hid[:, p, f * P:(f + 1) * P], ident[:])
                last.then_inc(hidT_psum, 1)

            def down(j, p, first=False):
                e = expert_of(j)
                pe.wait_ge(hl_ready, j + 1)
                if not first:
                    pe.wait_ge(y_ready, j)
                for f in range(NF):
                    part = slice(f * P, (f + 1) * P)
                    at = e * (2 * WE) + (4 * F + 2 * f * C)
                    m.matmul(pe_y[:, 0:2 * C], hh[:, p, part], w_two[:, bass.ds(at, 2 * C)], start=f == 0, stop=False)
                    m.matmul(pe_y[:, 0:C], hl[:, p, part], w_two[:, bass.ds(at, C)], start=False, stop=False)
                last = m.matmul(pe_y[:, 0:C], sel[2][:], bias[:, bass.ds(e * C, C)], start=False, stop=True)
                last.then_inc(y_psum, 1)

            pe.wait_ge(offs_ready, 1)
            pe.wait_ge(whi_ready, E)
            pe.wait_ge(wlo_ready, E)
            pe.wait_ge(bias_back, 16)
            rows_T(0, 0, 16, first=True)
            rows_T(1, 1, 16)
            up(0, 0, first=True)
            rows_T(2, 0, 32)
            up(1, 1, first=True)
            hid_T(0, 0, first=True)
            rows_T(3, 1, 32)
            up(2, 0)
            hid_T(1, 1, first=True)
            down(0, 0, first=True)
            rows_T(4, 0, 48)
            up(3, 1)
            hid_T(2, 0)
            down(1, 1)
            with pe.Fori(0, (NS - 5) // 2) as jj:
                for s in range(2):
                    rows_T(2 * jj + (5 + s), (5 + s) % 2, 16 * jj + 48 + 16 * s)
                    up(2 * jj + (4 + s), s)
                    hid_T(2 * jj + (3 + s), (3 + s) % 2)
                    down(2 * jj + (2 + s), s)
            up(NS - 1, (NS - 1) % 2)
            hid_T(NS - 2, (NS - 2) % 2)
            down(NS - 3, (NS - 3) % 2)
            hid_T(NS - 1, (NS - 1) % 2)
            down(NS - 2, (NS - 2) % 2)
            down(NS - 1, (NS - 1) % 2)


def kernel(**inputs):
    import numpy as np
    import concourse.bacc as bacc
    from concourse.bass_utils import run_bass_kernel_spmd

    a = {k: np.asarray(v) for k, v in inputs.items()}
    B, T, C = a["L0_attn_x"].shape
    E, H, F = a["L0_ffn_w1"].shape
    P = 128
    w3 = a["L0_ffn_w3"].reshape(E, F // P, P, H).transpose(2, 0, 1, 3).reshape(P, E, F // P * H)
    laid = {
        "x": a["L0_attn_x"].reshape(T, C),
        "wkT": a["L0_attn_Wk"].T,
        "wvT": a["L0_attn_Wv"].T,
        "wrT": a["L0_attn_Wr"].T,
        "woT": a["L0_attn_Wo"].T,
        "cols": np.stack([a["L0_attn_time_decay"], a["L0_attn_time_first"], a["L0_attn_mix_k"].reshape(C),
                          a["L0_attn_mix_v"].reshape(C), a["L0_attn_mix_r"].reshape(C)], axis=1),
        "router": a["L0_ffn_router_w"],
        "wexp": np.concatenate([a["L0_ffn_w1"].transpose(1, 0, 2), a["L0_ffn_w2"].transpose(1, 0, 2), w3], axis=2),
        "b1": a["L0_ffn_b1"],
        "b2": a["L0_ffn_b2"],
        "b3": a["L0_ffn_b3"],
    }
    nc = bacc.Bacc("TRN2", target_bir_lowering=False, num_devices=1)
    arrays, args = {}, []
    for name, v in laid.items():
        v = np.ascontiguousarray(v)
        arrays[f"in_{name}"] = v
        args.append(nc.dram_tensor(f"in_{name}", v.shape, mybir.dt.from_np(v.dtype), kind="ExternalInput").ap())
    args.append(nc.dram_tensor("out_0", (T, C), mybir.dt.float32, kind="ExternalOutput").ap())
    rwkv_time_mix_then_routed_moe(nc, *args)
    r = run_bass_kernel_spmd(nc, [arrays], core_ids=[0])
    return r.results[0]["out_0"].reshape(B, T, C)
```

```python
import concourse.bass as bass
from concourse import mybir
from contextlib import ExitStack


def rwkv_time_mix_then_routed_moe(
    nc: bass.Bass,
    x_d: bass.AP,
    wkT_d: bass.AP,
    wvT_d: bass.AP,
    wrT_d: bass.AP,
    woT_d: bass.AP,
    cols_d: bass.AP,
    router_d: bass.AP,
    wexp_d: bass.AP,
    b1_d: bass.AP,
    b2_d: bass.AP,
    b3_d: bass.AP,
    out_d: bass.AP,
):
    f32, f32r, bf16, i32 = mybir.dt.float32, mybir.dt.float32r, mybir.dt.bfloat16, mybir.dt.int32
    ALU = mybir.AluOpType
    ACT = mybir.ActivationFunctionType
    AXX = mybir.AxisListType.X

    P = 128
    T, C = x_d.shape
    E = router_d.shape[1]
    F = b1_d.shape[1]
    K = 2
    NT = T // P
    CT = 4
    CW = CT * P
    NC = T // CW
    NF = F // P
    WE = 3 * F
    PIECES = 3 * E
    RING = 6
    NS = K * T // P + E - 1
    NSP = NS + NS % 2
    KN = K * NT
    EPS = 1e-5
    NEG = -1e38
    NB3 = E * C // P
    ROUND_UP = 0.496
    TO_INTEGER = 1.5 * 2 ** 23
    QUARTERS = 4

    xn2_d = nc.dram_tensor("xn2_rows", (T, C), f32, kind="Internal").ap()
    z_d = nc.dram_tensor("expert_rows", (K * T, C), f32, kind="Internal").ap()
    bias_d = nc.dram_tensor("bias_rows", (3, 2, E * F), f32, kind="Internal").ap()

    with ExitStack() as ctx:
        def sb(name, shape, dt=f32):
            return ctx.enter_context(nc.sbuf_tensor(name, shape, dt))

        def sem(name):
            return ctx.enter_context(nc.semaphore(name))

        ident = sb("ident", [P, P])
        ones = sb("ones", [P, 1 + E])
        ones_bf = sb("ones_bf", [P, P], bf16)
        spare = sb("spare", [P, 512], bf16)
        not_before = sb("not_before", [P, P], bf16)
        iota_f = sb("iota_f", [P, P])
        kn_id = sb("kn_id", [P, KN])
        p_id = sb("p_id", [P, 1])
        sel_tmp = sb("sel_tmp", [6, P])
        sel = [sb(f"sel{i}", [6, P], f32r) for i in range(3)]
        cols = sb("cols", [C, 5])
        omix = sb("omix", [C, 3])
        wdec = sb("wdec", [C, 1])
        wdec_row = sb("wdec_row", [C, CW])
        wT = sb("wT", [C, 4, C])
        wcur = sb("wcur", [C, 3, C])
        wprev = sb("wprev", [C, 3, C])
        router = sb("router", [C, E])
        w_raw = sb("w_raw", [P, RING, F])
        w_two = sb("w_two", [P, E * 2 * WE], f32r)
        b_raw = sb("b_raw", [P, 3, E * F // P])
        b_hi = sb("b_hi", [P, 3, E * F // P], f32r)
        b_lo = sb("b_lo", [P, 3, E * F // P], f32r)
        xs = sb("xs", [P, NT, C])
        stats = sb("stats", [P, 2 * NT, 6])
        mv = sb("mv", [P, 2 * NT, 2])
        eps = sb("eps", [P, 1])
        lnv = sb("lnv", [P, 2 * NT])
        rstd0 = sb("rstd0", [P, 2 * NT])
        nwt = sb("nwt", [P, 2 * NT])
        rstd = sb("rstd", [P, 2 * NT])
        nmr = sb("nmr", [P, 2 * NT])
        gates = sb("gates", [P, K, NT])
        te_i = sb("te_i", [1, NSP], i32)
        gat_i = sb("gat_i", [P, NSP], i32)
        sca_i = sb("sca_i", [P, NSP], i32)
        gat_now = sb("gat_now", [P, 2], i32)
        sca_now = sb("sca_now", [P, 2], i32)

        psum = [ctx.enter_context(nc.psum_tensor(f"bank{i}", [P, 512], f32)) for i in range(8)]

        ident_ready, consts_ready = sem("ident_ready"), sem("consts_ready")
        pool_step = sem("pool_step")
        cols_in, proj_in, router_in, bias_in = sem("cols_in"), sem("proj_in"), sem("router_in"), sem("bias_in")
        x_in = [sem(f"x_in{c}") for c in range(NC)]
        wdec_exp, mix_ready, wscaled = sem("wdec_exp"), sem("mix_ready"), sem("wscaled")
        w_in = [sem(f"w_in{i}") for i in range(RING)]
        whi_ready, wlo_ready = sem("whi_ready"), sem("wlo_ready")
        bhi_ready, blo_ready, bias_out, bias_back, bias_pad = (
            sem("bhi_ready"), sem("blo_ready"), sem("bias_out"), sem("bias_back"), sem("bias_pad"))
        stats_ready, aggr_ready, lnv_ready, rstd0_ready, newton, rstd_ready = (
            sem("stats_ready"), sem("aggr_ready"), sem("lnv_ready"),
            sem("rstd0_ready"), sem("newton"), sem("rstd_ready"))
        nmr_ready, qsum_ready = sem("nmr_ready"), sem("qsum_ready")
        xn_ready, xnT_psum, xnT_ready, xnT_pad = sem("xn_ready"), sem("xnT_psum"), sem("xnT_ready"), sem("xnT_pad")
        k_psum, v_psum, r_psum = sem("k_psum"), sem("v_psum"), sem("r_psum")
        k_ready, v_ready, absr, er_ready, softplus_ready, logsig_ready = (
            sem("k_ready"), sem("v_ready"), sem("absr"), sem("er_ready"), sem("softplus_ready"), sem("logsig_ready"))
        state_pad, m_ready, a_ready, b_ready, d_ready, dmin_ready, dmax_ready = (
            sem("state_pad"), sem("m_ready"), sem("a_ready"), sem("b_ready"), sem("d_ready"),
            sem("dmin_ready"), sem("dmax_ready"))
        ea_ready, eb_ready, e1_ready, e2_ready = sem("ea_ready"), sem("eb_ready"), sem("e1_ready"), sem("e2_ready")
        pv_ready, num_ready, den_ready, n1_ready, n2_ready, n_ready, q1_ready = (
            sem("pv_ready"), sem("num_ready"), sem("den_ready"), sem("n1_ready"), sem("n2_ready"),
            sem("n_ready"), sem("q1_ready"))
        lnq_ready, scale_log, scale_ready, rwkv_ready = (
            sem("lnq_ready"), sem("scale_log"), sem("scale_ready"), sem("rwkv_ready"))
        o_psum, x2_ready = sem("o_psum"), sem("x2_ready")
        xn2_ready, xn2_out = ([sem(f"{n}{c}") for c in range(NC)] for n in ("xn2_ready", "xn2_out"))
        xn2T_psum, xn2T_ready, logits_psum = sem("xn2T_psum"), sem("xn2T_ready"), sem("logits_psum")
        route, gate_log, exp_ready, mask_ready, rank_psum, lo_oh_ready, hi_oh_ready, hi_kn_ready, hi_p_ready, idx_psum = (
            sem("route"), sem("gate_log"), sem("exp_ready"), sem("mask_ready"), sem("rank_psum"), sem("lo_oh_ready"),
            sem("hi_oh_ready"), sem("hi_kn_ready"), sem("hi_p_ready"), sem("idx_psum"))
        gat_ready, sca_ready, pool_passed = sem("gat_ready"), sem("sca_ready"), sem("pool_passed")
        idx_ready, offs_ready = sem("idx_ready"), sem("offs_ready")
        rows_in = [sem("rows_in0"), sem("rows_in1")]
        rowsT_psum, xh_ready, xl_ready = sem("rowsT_psum"), sem("xh_ready"), sem("xl_ready")
        h1_psum, h2_psum, silu_ready, hid_ready = sem("h1_psum"), sem("h2_psum"), sem("silu_ready"), sem("hid_ready")
        hidT_psum, hh_ready, hl_ready = sem("hidT_psum"), sem("hh_ready"), sem("hl_ready")
        y_psum, y_ready = sem("y_psum"), sem("y_ready")
        y_out = [sem("y_out0"), sem("y_out1")]
        z_in = [[sem(f"z_in{k}_{c}") for c in range(NC)] for k in range(K)]
        z2_scaled = sem("z2_scaled")
        gates_ready, mixed, out_ready, out_stored = sem("gates_ready"), sem("mixed"), sem("out_ready"), sem("out_stored")

        def sp(name, shape, dt=f32):
            return phase.enter_context(nc.sbuf_tensor(name, shape, dt))

        with ExitStack() as phase:
            xn = sp("xn", [P, NC, CT, C])
            xnT = sp("xnT", [C, 1 + T])
            kk = sp("kk", [C, 2, CW])
            vv = sp("vv", [C, 2, CW])
            rr = sp("rr", [C, 2, CW])
            mst = sp("mst", [C, 1 + T])
            num = sp("num", [C, 1 + T])
            den = sp("den", [C, 1 + T])
            ea = sp("ea", [C, 2, CW])
            eb = sp("eb", [C, 2, CW])
            e1 = sp("e1", [C, 2, CW])
            e2 = sp("e2", [C, 2, CW])
            qq = sp("qq", [C, 2, CW])
            xn2T = sp("xn2T", [C, 2, CW])
        late = ctx.enter_context(ExitStack())
        phase = late
        bias = sp("bias", [6, E * F], f32r)
        with ExitStack() as phase:
            lo_oh = sp("lo_oh", [P, KN, P], bf16)
            hi_oh = sp("hi_oh", [P, KN, NSP], bf16)
            hi_kn = sp("hi_kn", [P, KN, NSP], bf16)
            hi_p = sp("hi_p", [P, KN, NSP], bf16)
            cand = sp("cand", [P, NT, E])
            rest = sp("rest", [P, NT, E])
            desc = sp("desc", [P, E])
            keep = sp("keep", [P, E, NT])
            top = [sp(f"top{k}", [P, NT]) for k in range(K)]
            choice = sp("choice", [P, NT])
            oh = sp("oh", [P, K, NT, E])
            mask = sp("mask", [P, E, NT], bf16)
            incl = sp("incl", [P, E, NT])
            pos = sp("pos", [P, E, NT])
            counts = sp("counts", [P, E])
            ntile = sp("ntile", [P, 1 + E])
            ends = sp("ends", [P, 1 + E])
            at = sp("at", [P, K, NT, E])
            slot = sp("slot", [P, KN])
            hi_f = sp("hi_f", [P, KN])
            lo_f = sp("lo_f", [P, KN])
            te_c = sp("te_c", [1, NSP, E - 1])
            te_f = sp("te_f", [1, NSP])
            id_i = sp("id_i", [P, NSP], i32)
            pr = sp("pr", [P, NT, 1 + E])
            total = sp("total", [P, NT])
        with ExitStack() as phase:
            rows = sp("rows", [P, 2, C])
            xh = sp("xh", [C, 2, P], f32r)
            xl = sp("xl", [C, 2, P], f32r)
            silu = sp("silu", [P, 2, F])
            hid = sp("hid", [P, 2, F])
            hh = sp("hh", [P, 2, F], f32r)
            hl = sp("hl", [P, 2, F], f32r)
            yrow = sp("yrow", [P, 2, C])
            zrow = sp("zrow", [P, K, NT, C])

        block = ctx.enter_context(nc.Block())

        ps_T, ps_K, ps_V, ps_O, ps_rank, ps_L = psum[0:6]
        ps_T2 = (ps_rank, ps_T)
        ps_R = psum[6:8]
        pe_rows, pe_y = psum[0], psum[7]
        pe_h1, pe_h2, pe_hT = psum[1:3], psum[3:5], psum[5:7]

        def tiles(buf, c):
            return buf[:, c * CT:(c + 1) * CT]

        def ln_tiles(g):
            if g < 2:
                return slice(CT, NT) if g else slice(0, CT)
            return slice(NT + (g - 2) * CT, NT + (g - 1) * CT)

        def ln_count(g):
            return ln_tiles(g).stop

        def raw_piece(k):
            raw = w_raw[:, k % RING]
            return raw if k % 3 < 2 else raw.rearrange("p (b c) -> p b c", c=C)

        def split_piece(k):
            part = w_two[:, k * 2 * F:(k + 1) * 2 * F]
            if k % 3 < 2:
                return part[:, 0:F], part[:, F:]
            part = part.rearrange("p (b h c) -> p h b c", h=2, c=C)
            return part[:, 0], part[:, 1]

        @block.sync
        def _(sp):
            def load_weights(k):
                if k >= RING:
                    sp.wait_ge(wlo_ready, k - RING + 1)
                sp.dma_start(w_raw[:, k % RING], wexp_d[:, k // 3, k % 3 * F:(k % 3 + 1) * F])\
                  .then_inc(w_in[k % RING], 16)

            def load_tokens(c):
                sp.dma_start(tiles(xs, c), x_d.rearrange("(n p) c -> p n c", p=P)[:, c * CT:(c + 1) * CT])\
                  .then_inc(x_in[c], 16)

            load_tokens(0)
            sp.dma_start(cols[:], cols_d).then_inc(cols_in, 16)
            load_tokens(1)
            for i, w in enumerate((wkT_d, wvT_d, wrT_d, woT_d)):
                sp.dma_start(wT[:, i], w).then_inc(proj_in, 16)
            load_tokens(2)
            load_tokens(3)
            for k in range(RING):
                load_weights(k)
            sp.dma_start(router[:], router_d).then_inc(router_in, 16)
            sp.dma_start(b_raw[:, 0], b1_d.rearrange("e (q f) -> (e q) f", q=P // E)).then_inc(bias_in, 16)
            sp.dma_start(b_raw[:, 1], b2_d.rearrange("e (q f) -> (e q) f", q=P // E)).then_inc(bias_in, 16)
            sp.dma_start(b_raw[:, 2, 0:NB3], b3_d.rearrange("e (q h) -> (e q) h", q=P // E))\
              .then_inc(bias_in, 16)
            sp.wait_ge(bhi_ready, 1)
            sp.wait_ge(blo_ready, 1)
            for h, b in enumerate((b_hi, b_lo)):
                part = b[:].bitcast(f32)
                sp.dma_start(bias_d[0:2, h].rearrange("b (p f) -> p b f", p=P), part[:, 0:2]).then_inc(bias_out, 16)
                sp.dma_start(bias_d[2, h, 0:E * C].rearrange("(p f) -> p f", p=P), part[:, 2, 0:NB3])\
                  .then_inc(bias_out, 16)
                sp.dma_start(bias_d[2, h, E * C:].rearrange("(p f) -> p f", p=P), part[:, 2, NB3:])\
                  .then_inc(bias_out, 16)
            for k in range(RING, PIECES):
                load_weights(k)
            sp.wait_ge(bias_out, 96)
            for c in range(NC):
                sp.wait_ge(xn2_out[c], 16)
            sp.dma_start(bias[:].bitcast(f32), bias_d.rearrange("b h f -> (b h) f")).then_inc(bias_back, 16)
            sp.wait_ge(y_out[0], 16 * ((NS + 1) // 2))
            sp.wait_ge(y_out[1], 16 * (NS // 2))
            for c in range(NC):
                for k in range(K):
                    sp.dma_start(tiles(zrow[:, k], c),
                                 z_d[k * T + c * CW:k * T + (c + 1) * CW].rearrange("(n p) c -> p n c", p=P))\
                      .then_inc(z_in[k][c], 16)
            for c in range(NC):
                sp.wait_ge(out_ready, c + 1)
                sp.dma_start(out_d.rearrange("(n p) c -> p n c", p=P)[:, c * CT:(c + 1) * CT], tiles(xs, c))\
                  .then_inc(out_stored, 16)
            sp.wait_ge(out_stored, 16 * NC)

        @block.gpsimd
        def _(pool):
            g = nc.gpsimd
            g.memset(eps[:], EPS).then_inc(pool_step, 1)
            g.memset(ident[:], 0.0).then_inc(pool_step, 1)
            g.memset(ones[:], 1.0).then_inc(pool_step, 1)
            g.memset(not_before[:], 0.0).then_inc(pool_step, 1)
            g.memset(ones_bf[:], 1.0).then_inc(pool_step, 1)
            pool.wait_ge(pool_step, 5)
            g.affine_select(out=ident[:], in_=ident[:], compare_op=ALU.not_equal, fill=1.0, base=0,
                            pattern=[[-1, P]], channel_multiplier=1).then_inc(pool_step, 1)
            g.affine_select(out=not_before[:], in_=not_before[:], compare_op=ALU.is_gt, fill=-1.0, base=0,
                            pattern=[[1, P]], channel_multiplier=-1).then_inc(pool_step, 1)
            g.iota(iota_f[:], pattern=[[1, P]], base=0, channel_multiplier=0,
                   allow_small_or_imprecise_dtypes=True).then_inc(pool_step, 1)
            g.iota(kn_id[:], pattern=[[P, KN]], base=0, channel_multiplier=0,
                   allow_small_or_imprecise_dtypes=True).then_inc(pool_step, 1)
            g.iota(p_id[:], pattern=[[0, 1]], base=1, channel_multiplier=1,
                   allow_small_or_imprecise_dtypes=True).then_inc(pool_step, 1)
            pool.wait_ge(pool_step, 10)
            g.memset(spare[:], 0.0).then_inc(pool_step, 1)
            pool.wait_ge(pool_step, 11)
            g.engine_nop().then_inc(ident_ready, 1)
            g.memset(xnT[:, 0:1], 0.0).then_inc(xnT_pad, 1)
            g.memset(mst[:, 0:1], NEG).then_inc(state_pad, 1)
            g.memset(num[:, 0:1], 0.0).then_inc(state_pad, 1)
            g.memset(den[:, 0:1], 0.0).then_inc(state_pad, 1)
            n = 11
            for i in range(3):
                g.memset(sel_tmp[:], 1.0).then_inc(pool_step, 1)
                n += 1
                pool.wait_ge(pool_step, n)
                g.affine_select(out=sel_tmp[:], in_=sel_tmp[:], compare_op=ALU.is_ge, fill=0.0, base=-2 * i,
                                pattern=[[0, P]], channel_multiplier=1).then_inc(pool_step, 1)
                n += 1
                pool.wait_ge(pool_step, n)
                g.affine_select(out=sel[i][:], in_=sel_tmp[:], compare_op=ALU.is_ge, fill=0.0, base=2 * i + 1,
                                pattern=[[0, P]], channel_multiplier=-1).then_inc(pool_step, 1)
                n += 1
                pool.wait_ge(pool_step, n)
            g.engine_nop().then_inc(consts_ready, 1)
            pool.wait_ge(bhi_ready, 1)
            g.tensor_tensor(b_lo[:], b_raw[:], b_hi[:].bitcast(f32), ALU.subtract).then_inc(blo_ready, 1)

            def weights_lo(k):
                pool.wait_ge(whi_ready, k + 1)
                hi, lo = split_piece(k)
                g.tensor_tensor(lo, raw_piece(k), hi.bitcast(f32), ALU.subtract).then_inc(wlo_ready, 1)

            def key_exponent(c):
                b = c % 2
                pool.wait_ge(m_ready, c + 1)
                if c >= 2:
                    pool.wait_ge(den_ready, c - 1)
                g.tensor_tensor(eb[:, b], kk[:, b], mst[:, 1 + c * CW:1 + (c + 1) * CW], ALU.subtract)\
                 .then_inc(b_ready, 1)

            def decay_exponent(c):
                pool.wait_ge(m_ready, c + 1)
                if c >= 2:
                    pool.wait_ge(den_ready, c - 1)
                    pool.wait_ge(num_ready, c - 1)
                g.tensor_tensor(ea[:, c % 2], mst[:, c * CW:(c + 1) * CW], mst[:, 1 + c * CW:1 + (c + 1) * CW],
                                ALU.subtract).then_inc(a_ready, 1)

            def state_value(c):
                b = c % 2
                pool.wait_ge(eb_ready, c + 1)
                pool.wait_ge(v_ready, c + 1)
                pool.wait_ge(d_ready, c + 1)
                g.tensor_tensor(kk[:, b], eb[:, b], vv[:, b], ALU.mult).then_inc(pv_ready, 1)

            def current_share(c):
                b = c % 2
                pool.wait_ge(e2_ready, c + 1)
                g.tensor_tensor(vv[:, b], e2[:, b], vv[:, b], ALU.mult).then_inc(n2_ready, 1)

            def add_shares(c):
                b = c % 2
                pool.wait_ge(n1_ready, c + 1)
                pool.wait_ge(n2_ready, c + 1)
                g.tensor_tensor(e1[:, b], e1[:, b], vv[:, b], ALU.add).then_inc(n_ready, 1)

            weights_lo(0)
            weights_lo(1)
            weights_lo(2)
            key_exponent(0)
            decay_exponent(0)
            state_value(0)
            decay_exponent(1)
            key_exponent(1)
            current_share(0)
            add_shares(0)
            state_value(1)
            current_share(1)
            decay_exponent(2)
            add_shares(1)
            key_exponent(2)
            state_value(2)
            decay_exponent(3)
            key_exponent(3)
            current_share(2)
            state_value(3)
            add_shares(2)
            current_share(3)
            weights_lo(3)
            weights_lo(4)
            weights_lo(5)
            add_shares(3)
            for k in range(6, PIECES):
                weights_lo(k)

            for h in range(2):
                part = slice(h * KN // 2, (h + 1) * KN // 2)
                pool.wait_ge(hi_oh_ready, h + 1)
                g.tensor_tensor(hi_kn[:, part], hi_oh[:, part],
                                kn_id[:, part].unsqueeze(2).broadcast_to([P, KN // 2, NSP]), ALU.mult)\
                 .then_inc(hi_kn_ready, 1)

            def gather(j, p, waits=True):
                if waits:
                    pool.wait_ge(rowsT_psum, j - 1)
                    pool.sem_inc(pool_passed, 1)
                g.tensor_copy(gat_now[:, p:p + 1], gat_i[:, bass.ds(j, 1)]).then_inc(gat_ready, 1)
                pool.wait_ge(gat_ready, j + 1)
                pool.sem_inc(pool_passed, 1)
                g.indirect_dma_start(
                    out=rows[:, p], out_offset=None, in_=xn2_d,
                    in_offset=bass.IndirectOffsetOnAxis(ap=gat_now[:, p:p + 1], axis=0))\
                 .then_inc(rows_in[p], 16)

            def scatter(j, p):
                pool.wait_ge(y_ready, j + 1)
                pool.sem_inc(pool_passed, 1)
                g.tensor_copy(sca_now[:, p:p + 1], sca_i[:, bass.ds(j, 1)]).then_inc(sca_ready, 1)
                pool.wait_ge(sca_ready, j + 1)
                pool.sem_inc(pool_passed, 1)
                g.indirect_dma_start(
                    out=z_d, out_offset=bass.IndirectOffsetOnAxis(ap=sca_now[:, p:p + 1], axis=0),
                    in_=yrow[:, p], in_offset=None, bounds_check=K * T - 1, oob_is_err=False)\
                 .then_inc(y_out[p], 16)

            pool.wait_ge(idx_ready, 2)
            for c in range(NC):
                pool.wait_ge(xn2_out[c], 16)
            LAG = 5
            for j in range(LAG):
                gather(j, j % 2, waits=j >= 2)
            assert (NS - LAG) % 2 == 0
            with pool.Fori(0, (NS - LAG) // 2) as jj:
                for s in range(2):
                    gather(2 * jj + (LAG + s), (LAG + s) % 2)
                    scatter(2 * jj + s, s)
            for j in range(NS - LAG, NS):
                scatter(j, j % 2)

        @block.scalar
        def _(act):
            a = nc.scalar
            act.preload_act_table_set("natural_log_exp_and_others")
            act.wait_ge(cols_in, 16)
            a.activation(wdec[:], cols[:, 0:1], ACT.Exp).then_inc(wdec_exp, 1)

            def inverse_root_guess(g):
                s, n = ln_tiles(g), g + 1
                act.wait_ge(aggr_ready, ln_count(g))
                act.wait_ge(ident_ready, 1)
                a.activation(lnv[:, s], mv[:, s, 1], ACT.Ln, bias=eps[:, 0:1]).then_inc(lnv_ready, 1)
                act.wait_ge(lnv_ready, n)
                a.activation(rstd0[:, s], lnv[:, s], ACT.Exp, scale=-0.5).then_inc(rstd0_ready, 1)

            def token_rows(c):
                act.wait_ge(nmr_ready, 1 + (c > 0))
                for t in range(c * CT, (c + 1) * CT):
                    a.activation(xn[:, c, t % CT], xs[:, t], ACT.Identity, bias=nmr[:, t:t + 1],
                                 scale=rstd[:, t:t + 1]).then_inc(xn_ready, 1)

            def token_columns(c):
                act.wait_ge(xnT_psum, c + 1)
                a.activation(xnT[:, 1 + c * CW:1 + (c + 1) * CW], ps_T[:], ACT.Copy).then_inc(xnT_ready, 1)

            def keys(c):
                act.wait_ge(k_psum, c + 1)
                if c >= 2:
                    act.wait_ge(num_ready, c - 1)
                a.activation(kk[:, c % 2], ps_K[:], ACT.Copy).then_inc(k_ready, 1)

            def values(c):
                act.wait_ge(v_psum, c + 1)
                if c >= 2:
                    act.wait_ge(n_ready, c - 1)
                a.activation(vv[:, c % 2], ps_V[:], ACT.Copy).then_inc(v_ready, 1)

            def receptance_magnitude(c):
                act.wait_ge(r_psum, c + 1)
                if c >= 2:
                    act.wait_ge(scale_log, c - 1)
                a.activation(rr[:, c % 2], ps_R[c % 2][:], ACT.Abs).then_inc(absr, 1)

            def receptance_exponential(c):
                act.wait_ge(absr, c + 1)
                a.activation(rr[:, c % 2], rr[:, c % 2], ACT.Exp, scale=-1.0).then_inc(er_ready, 1)

            def receptance_logarithm(c):
                act.wait_ge(er_ready, c + 1)
                a.activation(rr[:, c % 2], rr[:, c % 2], ACT.Ln, bias=1.0).then_inc(softplus_ready, 1)

            def weights_hi(k):
                act.wait_ge(w_in[k % RING], 16 * (k // RING + 1))
                a.activation(split_piece(k)[0], raw_piece(k), ACT.Copy).then_inc(whi_ready, 1)

            def decay_exponential(c):
                act.wait_ge(a_ready, c + 1)
                act.wait_ge(mix_ready, 2)
                a.activation(ea[:, c % 2], ea[:, c % 2], ACT.Exp, bias=wdec[:, 0:1]).then_inc(ea_ready, 1)

            def key_exponential(c):
                act.wait_ge(b_ready, c + 1)
                a.activation(eb[:, c % 2], eb[:, c % 2], ACT.Exp).then_inc(eb_ready, 1)

            def past_exponential(c):
                act.wait_ge(dmax_ready, c + 1)
                a.activation(e1[:, c % 2], e1[:, c % 2], ACT.Exp, scale=-1.0).then_inc(e1_ready, 1)

            def current_exponential(c):
                act.wait_ge(dmin_ready, c + 1)
                a.activation(e2[:, c % 2], e2[:, c % 2], ACT.Exp).then_inc(e2_ready, 1)

            def denominator_logarithm(c):
                act.wait_ge(qsum_ready, c + 1)
                a.activation(qq[:, c % 2], qq[:, c % 2], ACT.Ln).then_inc(lnq_ready, 1)

            def output_scale(c):
                act.wait_ge(scale_log, c + 1)
                a.activation(qq[:, c % 2], qq[:, c % 2], ACT.Exp).then_inc(scale_ready, 1)

            def second_rows(c):
                act.wait_ge(nmr_ready, 3 + c)
                for t in range(c * CT, (c + 1) * CT):
                    a.activation(xn[:, c, t % CT], xs[:, t], ACT.Identity, bias=nmr[:, NT + t:NT + t + 1],
                                 scale=rstd[:, NT + t:NT + t + 1]).then_inc(xn2_ready[c], 1)

            def second_columns(c):
                act.wait_ge(xn2T_psum, c + 1)
                if c >= 2:
                    act.wait_ge(logits_psum, c - 1)
                a.activation(xn2T[:, c % 2], ps_T2[c % 2][:], ACT.Copy).then_inc(xn2T_ready, 1)
                act.wait_ge(xn2_ready[c], CT)
                act.dma_start(xn2_d.rearrange("(n p) c -> p n c", p=P)[:, c * CT:(c + 1) * CT], xn[:, c])\
                   .then_inc(xn2_out[c], 16)

            inverse_root_guess(0)
            token_rows(0)
            token_columns(0)
            inverse_root_guess(1)
            weights_hi(0)
            weights_hi(1)
            act.wait_ge(bias_in, 48)
            act.wait_ge(bias_pad, 1)
            a.activation(b_hi[:], b_raw[:], ACT.Copy).then_inc(bhi_ready, 1)
            token_rows(1)
            keys(0)
            token_rows(2)
            weights_hi(2)
            token_columns(1)
            values(0)
            key_exponential(0)
            receptance_magnitude(0)
            decay_exponential(0)
            keys(1)
            past_exponential(0)
            current_exponential(0)
            receptance_exponential(0)
            token_rows(3)
            receptance_logarithm(0)
            decay_exponential(1)
            token_columns(2)
            denominator_logarithm(0)
            key_exponential(1)
            values(1)
            receptance_magnitude(1)
            past_exponential(1)
            receptance_exponential(1)
            output_scale(0)
            receptance_logarithm(1)
            current_exponential(1)
            keys(2)
            token_columns(3)
            denominator_logarithm(1)
            values(2)
            decay_exponential(2)
            output_scale(1)
            keys(3)
            receptance_magnitude(2)
            key_exponential(2)
            current_exponential(2)
            past_exponential(2)
            receptance_exponential(2)
            receptance_logarithm(2)
            values(3)
            weights_hi(3)
            decay_exponential(3)
            denominator_logarithm(2)
            key_exponential(3)
            receptance_magnitude(3)
            receptance_exponential(3)
            past_exponential(3)
            current_exponential(3)
            output_scale(2)
            receptance_logarithm(3)
            weights_hi(4)
            weights_hi(5)
            denominator_logarithm(3)
            weights_hi(6)
            weights_hi(7)
            weights_hi(8)
            inverse_root_guess(2)
            output_scale(3)
            second_rows(0)
            weights_hi(9)
            inverse_root_guess(3)
            weights_hi(10)
            weights_hi(11)
            second_columns(0)
            second_rows(1)
            inverse_root_guess(4)
            weights_hi(12)
            weights_hi(13)
            second_columns(1)
            inverse_root_guess(5)
            weights_hi(14)
            weights_hi(15)
            second_columns(2)
            weights_hi(16)
            second_columns(3)
            weights_hi(17)
            weights_hi(18)
            weights_hi(19)
            weights_hi(20)
            weights_hi(21)
            weights_hi(22)
            act.wait_ge(gate_log, 2)
            a.activation(pr[:], pr[:], ACT.Exp).then_inc(exp_ready, 1)
            weights_hi(PIECES - 1)
            for h in range(2):
                part = slice(h * KN // 2, (h + 1) * KN // 2)
                act.wait_ge(hi_oh_ready, h + 1)
                a.activation(hi_p[:, part], hi_oh[:, part], ACT.Copy, scale=p_id[:, 0:1]).then_inc(hi_p_ready, 1)
            act.preload_act_table_set("silu_and_others")

            def x_hi(j, p, first=False):
                act.wait_ge(rowsT_psum, j + 1)
                if not first:
                    act.wait_ge(h2_psum, j - 1)
                a.activation(xh[:, p], pe_rows[:, 0:P], ACT.Copy).then_inc(xh_ready, 1)

            def silu_of(j, p, first=False):
                act.wait_ge(h1_psum, j + 1)
                if not first:
                    act.wait_ge(hid_ready, j - 1)
                a.activation(silu[:, p], pe_h1[p][:], ACT.Silu).then_inc(silu_ready, 1)

            def hid_hi(j, p, first=False):
                act.wait_ge(hidT_psum, j + 1)
                if not first:
                    act.wait_ge(y_psum, j - 1)
                a.activation(hh[:, p], pe_hT[p][:], ACT.Copy).then_inc(hh_ready, 1)

            x_hi(0, 0, first=True)
            x_hi(1, 1, first=True)
            silu_of(0, 0, first=True)
            x_hi(2, 0)
            silu_of(1, 1, first=True)
            hid_hi(0, 0, first=True)
            x_hi(3, 1)
            silu_of(2, 0)
            hid_hi(1, 1, first=True)
            with act.Fori(0, (NS - 5) // 2) as jj:
                for s in range(2):
                    x_hi(2 * jj + (4 + s), s)
                    silu_of(2 * jj + (3 + s), (3 + s) % 2)
                    hid_hi(2 * jj + (2 + s), s)
            x_hi(NS - 1, (NS - 1) % 2)
            silu_of(NS - 2, (NS - 2) % 2)
            hid_hi(NS - 3, (NS - 3) % 2)
            silu_of(NS - 1, (NS - 1) % 2)
            hid_hi(NS - 2, (NS - 2) % 2)
            hid_hi(NS - 1, (NS - 1) % 2)
            act.wait_ge(gates_ready, 1)
            for c in range(NC):
                act.wait_ge(z_in[1][c], 16)
                for t in range(c * CT, (c + 1) * CT):
                    a.activation(zrow[:, 1, t], zrow[:, 1, t], ACT.Copy, scale=gates[:, 1, t:t + 1])\
                     .then_inc(z2_scaled, 1)

        @block.vector
        def _(dve):
            v = nc.vector

            def statistics(g):
                s = ln_tiles(g)
                for t in range(s.start, s.stop):
                    v.bn_stats(stats[:, t], xs[:, t % NT]).then_inc(stats_ready, 1)

            def aggregate(g):
                s, n = ln_tiles(g), ln_count(g)
                dve.wait_ge(stats_ready, n)
                for t in range(s.start, s.stop):
                    v.bn_aggr(mv[:, t], stats[:, t]).then_inc(aggr_ready, 1)

            def newton_step(g):
                s, n = ln_tiles(g), g + 1
                dve.wait_ge(rstd0_ready, n)
                v.scalar_tensor_tensor(nwt[:, s], rstd0[:, s], -0.5, rstd0[:, s], ALU.mult, ALU.mult)\
                 .then_inc(newton, 1)
                dve.wait_ge(newton, 2 * n - 1)
                v.scalar_tensor_tensor(nwt[:, s], mv[:, s, 1], EPS, nwt[:, s], ALU.add, ALU.mult).then_inc(newton, 1)
                dve.wait_ge(newton, 2 * n)
                v.scalar_tensor_tensor(rstd[:, s], nwt[:, s], 1.5, rstd0[:, s], ALU.add, ALU.mult)\
                 .then_inc(rstd_ready, 1)
                dve.wait_ge(rstd_ready, n)
                v.scalar_tensor_tensor(nmr[:, s], mv[:, s, 0], -1.0, rstd[:, s], ALU.mult, ALU.mult)\
                 .then_inc(nmr_ready, 1)

            def prepare_decay():
                dve.wait_ge(wdec_exp, 1)
                v.tensor_scalar(wdec[:], wdec[:], -1.0, None, ALU.mult).then_inc(mix_ready, 1)
                v.memset(wdec_row[:], 0.0).then_inc(mix_ready, 1)
                dve.wait_ge(mix_ready, 2)
                v.tensor_scalar(wdec_row[:], wdec_row[:], wdec[:, 0:1], None, ALU.add).then_inc(mix_ready, 1)

            def prepare_projections():
                v.tensor_scalar(omix[:], cols[:, 2:5], -1.0, 1.0, ALU.mult, ALU.add).then_inc(mix_ready, 1)
                dve.wait_ge(mix_ready, 4)
                dve.wait_ge(proj_in, 64)
                for i in range(3):
                    v.tensor_scalar(wcur[:, i], wT[:, i], cols[:, 2 + i:3 + i], None, ALU.mult).then_inc(wscaled, 1)
                    v.tensor_scalar(wprev[:, i], wT[:, i], omix[:, i:i + 1], None, ALU.mult).then_inc(wscaled, 1)

            def now(c):
                return slice(1 + c * CW, 1 + (c + 1) * CW)

            def before(c):
                return slice(c * CW, (c + 1) * CW)

            def running_maximum(c):
                dve.wait_ge(k_ready, c + 1)
                v.tensor_tensor_scan(mst[:, now(c)], wdec_row[:], kk[:, c % 2], mst[:, c * CW:c * CW + 1],
                                     ALU.add, ALU.max).then_inc(m_ready, 1)

            def output_exponent(c):
                dve.wait_ge(m_ready, c + 1)
                if c >= 2:
                    dve.wait_ge(o_psum, c - 1)
                v.scalar_tensor_tensor(e1[:, c % 2], kk[:, c % 2], cols[:, 1:2], mst[:, before(c)], ALU.add, ALU.subtract)\
                 .then_inc(d_ready, 1)

            def d_min(c):
                dve.wait_ge(d_ready, c + 1)
                if c >= 2:
                    dve.wait_ge(n2_ready, c - 1)
                v.tensor_scalar(e2[:, c % 2], e1[:, c % 2], 0.0, None, ALU.min).then_inc(dmin_ready, 1)

            def d_max(c):
                v.tensor_scalar(e1[:, c % 2], e1[:, c % 2], 0.0, None, ALU.max).then_inc(dmax_ready, 1)

            def denominator(c):
                dve.wait_ge(ea_ready, c + 1)
                dve.wait_ge(eb_ready, c + 1)
                v.tensor_tensor_scan(den[:, now(c)], ea[:, c % 2], eb[:, c % 2], den[:, c * CW:c * CW + 1],
                                     ALU.mult, ALU.add).then_inc(den_ready, 1)

            def numerator(c):
                dve.wait_ge(pv_ready, c + 1)
                v.tensor_tensor_scan(num[:, now(c)], ea[:, c % 2], kk[:, c % 2], num[:, c * CW:c * CW + 1],
                                     ALU.mult, ALU.add).then_inc(num_ready, 1)

            def past_denominator(c):
                dve.wait_ge(e1_ready, c + 1)
                dve.wait_ge(den_ready, c + 1)
                v.tensor_tensor(qq[:, c % 2], e1[:, c % 2], den[:, before(c)], ALU.mult).then_inc(q1_ready, 1)

            def output_denominator(c):
                dve.wait_ge(q1_ready, c + 1)
                dve.wait_ge(e2_ready, c + 1)
                v.tensor_tensor(qq[:, c % 2], e2[:, c % 2], qq[:, c % 2], ALU.add).then_inc(qsum_ready, 1)

            def past_numerator(c):
                dve.wait_ge(num_ready, c + 1)
                v.tensor_tensor(e1[:, c % 2], e1[:, c % 2], num[:, before(c)], ALU.mult).then_inc(n1_ready, 1)

            def log_sigmoid(c):
                dve.wait_ge(softplus_ready, c + 1)
                v.scalar_tensor_tensor(rr[:, c % 2], ps_R[c % 2][:], 0.0, rr[:, c % 2], ALU.min, ALU.subtract)\
                 .then_inc(logsig_ready, 1)

            def output_scale_log(c):
                dve.wait_ge(lnq_ready, c + 1)
                dve.wait_ge(logsig_ready, c + 1)
                v.tensor_tensor(qq[:, c % 2], rr[:, c % 2], qq[:, c % 2], ALU.subtract).then_inc(scale_log, 1)

            def output(c):
                dve.wait_ge(scale_ready, c + 1)
                dve.wait_ge(n_ready, c + 1)
                v.tensor_tensor(e1[:, c % 2], e1[:, c % 2], qq[:, c % 2], ALU.mult).then_inc(rwkv_ready, 1)

            def residual(c):
                dve.wait_ge(o_psum, c + 1)
                v.tensor_tensor(tiles(xs, c), ps_O[:].rearrange("p (t c) -> p t c", c=C), tiles(xs, c),
                                ALU.add).then_inc(x2_ready, 1)

            def second_statistics(c):
                dve.wait_ge(x2_ready, c + 1)
                statistics(2 + c)

            def second_rows(c):
                dve.wait_ge(nmr_ready, 3 + c)
                dve.wait_ge(xnT_psum, NC)
                for t in range(c * CT, (c + 1) * CT):
                    v.tensor_scalar(xn[:, c, t % CT], xs[:, t], rstd[:, NT + t:NT + t + 1],
                                    nmr[:, NT + t:NT + t + 1], ALU.mult, ALU.add).then_inc(xn2_ready[c], 1)

            dve.wait_ge(x_in[0], 16)
            statistics(0)
            aggregate(0)
            newton_step(0)
            dve.wait_ge(cols_in, 16)
            prepare_decay()
            prepare_projections()
            for c in range(1, NC):
                dve.wait_ge(x_in[c], 16)
            statistics(1)
            aggregate(1)
            newton_step(1)
            v.memset(b_raw[:, 2, NB3:], 0.0).then_inc(bias_pad, 1)
            dve.wait_ge(state_pad, 3)
            running_maximum(0)
            output_exponent(0)
            d_min(0)
            d_max(0)
            denominator(0)
            running_maximum(1)
            past_denominator(0)
            numerator(0)
            output_exponent(1)
            output_denominator(0)
            d_min(1)
            log_sigmoid(0)
            past_numerator(0)
            d_max(1)
            output_scale_log(0)
            denominator(1)
            past_denominator(1)
            numerator(1)
            output(0)
            output_denominator(1)
            running_maximum(2)
            log_sigmoid(1)
            past_numerator(1)
            output_scale_log(1)
            output_exponent(2)
            output(1)
            d_min(2)
            residual(0)
            d_max(2)
            running_maximum(3)
            denominator(2)
            past_denominator(2)
            output_exponent(3)
            output_denominator(2)
            d_min(3)
            numerator(2)
            log_sigmoid(2)
            past_numerator(2)
            d_max(3)
            denominator(3)
            output_scale_log(2)
            past_denominator(3)
            second_statistics(0)
            output(2)
            numerator(3)
            residual(1)
            output_denominator(3)
            past_numerator(3)
            aggregate(2)
            log_sigmoid(3)
            output_scale_log(3)
            newton_step(2)
            second_statistics(1)
            residual(2)
            aggregate(3)
            output(3)
            newton_step(3)
            second_statistics(2)
            aggregate(4)
            residual(3)
            second_statistics(3)
            newton_step(4)
            aggregate(5)
            second_rows(2)
            newton_step(5)
            second_rows(3)

            n = [0]

            def step(ins):
                n[0] += 1
                ins.then_inc(route, 1)
                dve.wait_ge(route, n[0])

            def over_e(t):
                return t.unsqueeze(2).broadcast_to([P, NT, E])

            logits = ps_L[:, 0:NT * E].rearrange("p (n e) -> p n e", e=E)
            step(v.memset(keep[:], 1.0))
            step(v.memset(keep[:, :, 0:1], 0.0))
            step(v.memset(ntile[:, 0:1], 0.0))
            step(v.tensor_scalar(desc[:], iota_f[:, 0:E], -1.0, float(E), ALU.mult, ALU.add))
            dve.wait_ge(logits_psum, NC)
            for k in range(K):
                score = logits if k == 0 else rest[:]
                step(v.tensor_reduce(top[k][:], score, AXX, ALU.max))
                step(v.tensor_tensor(cand[:], score, over_e(top[k][:]), ALU.is_equal))
                step(v.tensor_tensor(cand[:], cand[:], desc[:].unsqueeze(1).broadcast_to([P, NT, E]), ALU.mult))
                step(v.tensor_reduce(choice[:], cand[:], AXX, ALU.max))
                step(v.tensor_tensor(oh[:, k], cand[:], over_e(choice[:]), ALU.is_equal))
                if k == 0:
                    step(v.scalar_tensor_tensor(rest[:], oh[:, 0], NEG, logits, ALU.mult, ALU.add))
            v.tensor_tensor(mask[:], oh[:, 0].rearrange("p n e -> p e n"), oh[:, 1].rearrange("p n e -> p e n"),
                            ALU.add).then_inc(mask_ready, 1)
            v.tensor_tensor(pr[:, :, 0:E], logits, over_e(top[0][:]), ALU.subtract).then_inc(gate_log, 1)
            v.tensor_tensor(pr[:, :, E], top[1][:], top[0][:], ALU.subtract).then_inc(gate_log, 1)
            dve.wait_ge(rank_psum, 1)
            flat = "p e n -> p (e n)"
            step(v.tensor_tensor_scan(incl[:].rearrange(flat), keep[:].rearrange(flat), ps_K[:, 0:E * NT],
                                      0.0, ALU.mult, ALU.add))
            step(v.tensor_scalar(counts[:], incl[:, :, NT - 1], 1.0 / P, ROUND_UP, ALU.mult, ALU.add))
            step(v.tensor_scalar(ntile[:, 1:], counts[:], TO_INTEGER, TO_INTEGER, ALU.add, ALU.subtract))
            v.tensor_tensor(pos[:].rearrange(flat), ps_rank[:, 0:E * NT], incl[:].rearrange(flat), ALU.add)\
             .then_inc(route, 1)
            n[0] += 1
            step(v.tensor_tensor_scan(ends[:], ones[:, 0:1 + E], ntile[:], 0.0, ALU.mult, ALU.add))
            step(v.scalar_tensor_tensor(pos[:], ends[:, 0:E].unsqueeze(2).broadcast_to([P, E, NT]), float(P), pos[:],
                                        ALU.mult, ALU.add))
            step(v.tensor_tensor(at[:], oh[:], pos[:].rearrange("p e n -> p n e").unsqueeze(1)
                                 .broadcast_to([P, K, NT, E]), ALU.mult))
            step(v.tensor_reduce(slot[:].rearrange("p (k n) -> p k n", k=K), at[:], AXX, ALU.add))
            step(v.tensor_scalar(hi_f[:], slot[:], 1.0 / P, -ROUND_UP, ALU.mult, ALU.add))
            step(v.tensor_scalar(hi_f[:], hi_f[:], TO_INTEGER, TO_INTEGER, ALU.add, ALU.subtract))
            for h in range(2):
                part = slice(h * KN // 2, (h + 1) * KN // 2)
                v.tensor_tensor(hi_oh[:, part], iota_f[:, 0:NSP].unsqueeze(1).broadcast_to([P, KN // 2, NSP]),
                                hi_f[:, part].unsqueeze(2).broadcast_to([P, KN // 2, NSP]), ALU.is_equal)\
                 .then_inc(hi_oh_ready, 1)
                if h == 0:
                    v.scalar_tensor_tensor(lo_f[:], hi_f[:], -float(P), slot[:], ALU.mult, ALU.add).then_inc(route, 1)
                    n[0] += 1
            dve.wait_ge(route, n[0])
            for k in range(QUARTERS):
                part = slice(k * KN // QUARTERS, (k + 1) * KN // QUARTERS)
                v.tensor_tensor(lo_oh[:, part], iota_f[:].unsqueeze(1).broadcast_to([P, KN // QUARTERS, P]),
                                lo_f[:, part].unsqueeze(2).broadcast_to([P, KN // QUARTERS, P]), ALU.is_equal)\
                 .then_inc(lo_oh_ready, 1)
            step(v.tensor_tensor(te_c[:], iota_f[0:1, 0:NSP].unsqueeze(2).broadcast_to([1, NSP, E - 1]),
                                 ends[0:1, 1:E].unsqueeze(1).broadcast_to([1, NSP, E - 1]), ALU.is_ge))
            step(v.tensor_reduce(te_f[:], te_c[:], AXX, ALU.add))
            v.tensor_copy(te_i[:], te_f[:]).then_inc(offs_ready, 1)
            dve.wait_ge(idx_psum, 1)
            step(v.tensor_scalar(id_i[:], ps_L[:, 256:256 + NSP], -1.0, None, ALU.add))
            v.tensor_scalar(gat_i[:], id_i[:], T - 1, None, ALU.bitwise_and).then_inc(idx_ready, 1)
            v.tensor_scalar(sca_i[:], id_i[:], 4 * K * T - 1, None, ALU.bitwise_and).then_inc(idx_ready, 1)
            dve.wait_ge(exp_ready, 1)
            step(v.tensor_reduce(total[:], pr[:, :, 0:E], AXX, ALU.add))
            step(v.reciprocal(gates[:, 0], total[:]))
            v.tensor_tensor(gates[:, 1], pr[:, :, E], gates[:, 0], ALU.mult).then_inc(gates_ready, 1)

            def x_lo(j, p):
                dve.wait_ge(xh_ready, j + 1)
                v.tensor_tensor(xl[:, p], pe_rows[:, 0:P], xh[:, p].bitcast(f32), ALU.subtract)\
                 .then_inc(xl_ready, 1)

            def hidden(j, p, first=False):
                dve.wait_ge(silu_ready, j + 1)
                dve.wait_ge(h2_psum, j + 1)
                if not first:
                    dve.wait_ge(hidT_psum, j - 1)
                v.tensor_tensor(hid[:, p], silu[:, p], pe_h2[p][:], ALU.mult).then_inc(hid_ready, 1)

            def hid_lo(j, p):
                dve.wait_ge(hh_ready, j + 1)
                v.tensor_tensor(hl[:, p], pe_hT[p][:], hh[:, p].bitcast(f32), ALU.subtract).then_inc(hl_ready, 1)

            def y_copy(j, p, scattered=None):
                dve.wait_ge(y_psum, j + 1)
                if scattered is not None:
                    dve.wait_ge(y_out[p], scattered)
                v.tensor_reduce(yrow[:, p], pe_y[:, 0:2 * C].rearrange("p (h c) -> p c h", h=2), AXX, ALU.add)\
                 .then_inc(y_ready, 1)

            x_lo(0, 0)
            x_lo(1, 1)
            hidden(0, 0, first=True)
            x_lo(2, 0)
            hidden(1, 1, first=True)
            hid_lo(0, 0)
            x_lo(3, 1)
            hidden(2, 0)
            hid_lo(1, 1)
            y_copy(0, 0)
            x_lo(4, 0)
            hidden(3, 1)
            hid_lo(2, 0)
            y_copy(1, 1)
            with dve.Fori(0, (NS - 7) // 2) as jj:
                for s in range(2):
                    x_lo(2 * jj + (5 + s), (5 + s) % 2)
                    hidden(2 * jj + (4 + s), s)
                    hid_lo(2 * jj + (3 + s), (3 + s) % 2)
                    y_copy(2 * jj + (2 + s), s, scattered=16 * jj + 16)
            for j in range(NS - 3, NS + 2):
                if j + 1 < NS:
                    x_lo(j + 1, (j + 1) % 2)
                if j < NS:
                    hidden(j, j % 2)
                if j - 1 < NS:
                    hid_lo(j - 1, (j - 1) % 2)
                y_copy(j - 2, j % 2, scattered=16 * ((j - 2) // 2))

            dve.wait_ge(gates_ready, 1)
            for c in range(NC):
                dve.wait_ge(z_in[0][c], 16)
                for t in range(c * CT, (c + 1) * CT):
                    v.scalar_tensor_tensor(xs[:, t], zrow[:, 0, t], gates[:, 0, t:t + 1], xs[:, t],
                                           ALU.mult, ALU.add).then_inc(mixed, 1)
                dve.wait_ge(mixed, CT * (c + 1))
                dve.wait_ge(z2_scaled, CT * (c + 1))
                v.tensor_tensor(tiles(xs, c), tiles(xs, c), tiles(zrow[:, 1], c), ALU.add).then_inc(out_ready, 1)

        @block.tensor
        def _(pe):
            m = nc.tensor

            def keep_clock(n, bank):
                for _ in range(n):
                    m.matmul(bank[:], ones_bf[:], spare[:], start=True, stop=True)

            pe.wait_ge(ident_ready, 1)
            keep_clock(12, ps_O)

            def rows_to_channels(c):
                if c:
                    pe.wait_ge(xnT_ready, c)
                for t in range(CT):
                    pe.wait_ge(xn_ready, c * CT + t + 1)
                    last = m.transpose(ps_T[:, t * P:(t + 1) * P], xn[:, c, t], ident[:])
                last.then_inc(xnT_psum, 1)

            def project(c, w):
                bank, done, free, n = ((ps_K, k_psum, k_ready, c), (ps_V, v_psum, v_ready, c),
                                       (ps_R[c % 2], r_psum, logsig_ready, c - 1))[w]
                pe.wait_ge(xnT_ready, c + 1)
                if n >= 1:
                    pe.wait_ge(free, n)
                m.matmul(bank[:], wcur[:, w], xnT[:, 1 + c * CW:1 + (c + 1) * CW], start=True, stop=False)
                m.matmul(bank[:], wprev[:, w], xnT[:, c * CW:(c + 1) * CW], start=False, stop=True).then_inc(done, 1)

            KEYS, VALUES, RECEPTANCES = range(3)

            def project_output(c):
                pe.wait_ge(rwkv_ready, c + 1)
                if c:
                    pe.wait_ge(x2_ready, c)
                for t in range(CT):
                    last = m.matmul(ps_O[:, t * C:(t + 1) * C], e1[:, c % 2, t * P:(t + 1) * P], wT[:, 3],
                                    start=True, stop=True)
                last.then_inc(o_psum, 1)

            def second_to_channels(c):
                if c >= 2:
                    pe.wait_ge(xn2T_ready, c - 1)
                for t in range(CT):
                    pe.wait_ge(xn2_ready[c], t + 1)
                    last = m.transpose(ps_T2[c % 2][:, t * P:(t + 1) * P], xn[:, c, t], ident[:])
                last.then_inc(xn2T_psum, 1)

            def router_logits(c):
                pe.wait_ge(xn2T_ready, c + 1)
                for t in range(CT):
                    n = (c * CT + t) * E
                    last = m.matmul(ps_L[:, n:n + E], xn2T[:, c % 2, t * P:(t + 1) * P], router[:], start=True, stop=True)
                last.then_inc(logits_psum, 1)

            rows_to_channels(0)
            pe.wait_ge(wscaled, 6)
            pe.wait_ge(xnT_pad, 1)
            project(0, KEYS)
            project(0, VALUES)
            rows_to_channels(1)
            project(0, RECEPTANCES)
            project(1, KEYS)
            project(1, VALUES)
            rows_to_channels(2)
            project(1, RECEPTANCES)
            project(2, KEYS)
            rows_to_channels(3)
            project(2, VALUES)
            project_output(0)
            project(3, KEYS)
            project(2, RECEPTANCES)
            project(3, VALUES)
            project_output(1)
            project(3, RECEPTANCES)
            keep_clock(22, ps_L)
            project_output(2)
            pe.wait_ge(router_in, 16)
            second_to_channels(0)
            project_output(3)
            router_logits(0)
            second_to_channels(1)
            router_logits(1)
            second_to_channels(2)
            second_to_channels(3)
            router_logits(2)
            router_logits(3)
            pe.wait_ge(mask_ready, 1)
            m.matmul(ps_K[:, 0:E * NT], ones_bf[:], mask[:].rearrange("p e n -> p (e n)"), start=True, stop=True)
            m.matmul(ps_rank[:, 0:E * NT], not_before[:], mask[:].rearrange("p e n -> p (e n)"), start=True, stop=True)\
             .then_inc(rank_psum, 1)
            for kn in range(KN):
                if kn % (KN // QUARTERS) == 0:
                    pe.wait_ge(lo_oh_ready, kn // (KN // QUARTERS) + 1)
                    pe.wait_ge(hi_kn_ready, kn // (KN // 2) + 1)
                    pe.wait_ge(hi_p_ready, kn // (KN // 2) + 1)
                for rows_id in (hi_kn, hi_p):
                    last = m.matmul(ps_L[:, 256:256 + NSP], lo_oh[:, kn], rows_id[:, kn],
                                    start=kn == 0 and rows_id is hi_kn, stop=kn == KN - 1 and rows_id is hi_p)
            last.then_inc(idx_psum, 1)
            keep_clock(10, ps_R[0])

            def expert_of(j):
                _, (e,) = nc.values_load_multi_w_load_instructions(
                    te_i[0:1, bass.ds(j, 1)], engines=[mybir.EngineType.PE], min_val=0, max_val=E - 1,
                    skip_runtime_bounds_check_because="it is a count over E - 1 comparisons")
                return e

            def rows_T(j, p, landed, first=False):
                pe.wait_ge(rows_in[p], landed)
                if not first:
                    pe.wait_ge(xl_ready, j)
                m.transpose(pe_rows[:, 0:P], rows[:, p], ident[:]).then_inc(rowsT_psum, 1)

            def up(j, p, first=False):
                e = expert_of(j)
                pe.wait_ge(xl_ready, j + 1)
                for h, (bank, done, free) in enumerate(((pe_h1, h1_psum, silu_ready), (pe_h2, h2_psum, hid_ready))):
                    if not first:
                        pe.wait_ge(free, j - 1)
                    hi, lo = (w_two[:, bass.ds(e * (2 * WE) + (2 * h + i) * F, F)] for i in range(2))
                    m.matmul(bank[p][:], xh[:, p], hi, start=True, stop=False)
                    m.matmul(bank[p][:], sel[h][:], bias[:, bass.ds(e * F, F)], start=False, stop=False)
                    m.matmul(bank[p][:], xh[:, p], lo, start=False, stop=False)
                    m.matmul(bank[p][:], xl[:, p], hi, start=False, stop=True)\
                     .then_inc(done, 1)

            def hid_T(j, p, first=False):
                pe.wait_ge(hid_ready, j + 1)
                if not first:
                    pe.wait_ge(hl_ready, j - 1)
                for f in range(NF):
                    last = m.transpose(pe_hT[p][:, f * P:(f + 1) * P], hid[:, p, f * P:(f + 1) * P], ident[:])
                last.then_inc(hidT_psum, 1)

            def down(j, p, first=False):
                e = expert_of(j)
                pe.wait_ge(hl_ready, j + 1)
                if not first:
                    pe.wait_ge(y_ready, j)
                for f in range(NF):
                    part = slice(f * P, (f + 1) * P)
                    at = e * (2 * WE) + (4 * F + 2 * f * C)
                    m.matmul(pe_y[:, 0:2 * C], hh[:, p, part], w_two[:, bass.ds(at, 2 * C)], start=f == 0, stop=False)
                    m.matmul(pe_y[:, 0:C], hl[:, p, part], w_two[:, bass.ds(at, C)], start=False, stop=False)
                last = m.matmul(pe_y[:, 0:C], sel[2][:], bias[:, bass.ds(e * C, C)], start=False, stop=True)
                last.then_inc(y_psum, 1)

            pe.wait_ge(offs_ready, 1)
            pe.wait_ge(whi_ready, PIECES)
            pe.wait_ge(wlo_ready, PIECES)
            pe.wait_ge(bias_back, 16)
            rows_T(0, 0, 16, first=True)
            keep_clock(5, ps_R[0])
            rows_T(1, 1, 16)
            keep_clock(1, ps_R[0])
            up(0, 0, first=True)
            rows_T(2, 0, 32)
            up(1, 1, first=True)
            hid_T(0, 0, first=True)
            rows_T(3, 1, 32)
            up(2, 0)
            hid_T(1, 1, first=True)
            down(0, 0, first=True)
            rows_T(4, 0, 48)
            up(3, 1)
            hid_T(2, 0)
            down(1, 1)
            with pe.Fori(0, (NS - 5) // 2) as jj:
                for s in range(2):
                    rows_T(2 * jj + (5 + s), (5 + s) % 2, 16 * jj + 48 + 16 * s)
                    up(2 * jj + (4 + s), s)
                    hid_T(2 * jj + (3 + s), (3 + s) % 2)
                    down(2 * jj + (2 + s), s)
            up(NS - 1, (NS - 1) % 2)
            hid_T(NS - 2, (NS - 2) % 2)
            down(NS - 3, (NS - 3) % 2)
            hid_T(NS - 1, (NS - 1) % 2)
            down(NS - 2, (NS - 2) % 2)
            down(NS - 1, (NS - 1) % 2)


def kernel(**inputs):
    import numpy as np
    import concourse.bacc as bacc
    from concourse.bass_utils import run_bass_kernel_spmd

    a = {k: np.asarray(v) for k, v in inputs.items()}
    B, T, C = a["L0_attn_x"].shape
    E, H, F = a["L0_ffn_w1"].shape
    P = 128
    w3 = a["L0_ffn_w3"].reshape(E, F // P, P, H).transpose(2, 0, 1, 3).reshape(P, E, F // P * H)
    laid = {
        "x": a["L0_attn_x"].reshape(T, C),
        "wkT": a["L0_attn_Wk"].T,
        "wvT": a["L0_attn_Wv"].T,
        "wrT": a["L0_attn_Wr"].T,
        "woT": a["L0_attn_Wo"].T,
        "cols": np.stack([a["L0_attn_time_decay"], a["L0_attn_time_first"], a["L0_attn_mix_k"].reshape(C),
                          a["L0_attn_mix_v"].reshape(C), a["L0_attn_mix_r"].reshape(C)], axis=1),
        "router": a["L0_ffn_router_w"],
        "wexp": np.concatenate([a["L0_ffn_w1"].transpose(1, 0, 2), a["L0_ffn_w2"].transpose(1, 0, 2), w3], axis=2),
        "b1": a["L0_ffn_b1"],
        "b2": a["L0_ffn_b2"],
        "b3": a["L0_ffn_b3"],
    }
    nc = bacc.Bacc("TRN2", target_bir_lowering=False, num_devices=1)
    arrays, args = {}, []
    for name, v in laid.items():
        v = np.ascontiguousarray(v)
        arrays[f"in_{name}"] = v
        args.append(nc.dram_tensor(f"in_{name}", v.shape, mybir.dt.from_np(v.dtype), kind="ExternalInput").ap())
    args.append(nc.dram_tensor("out_0", (T, C), mybir.dt.float32, kind="ExternalOutput").ap())
    rwkv_time_mix_then_routed_moe(nc, *args)
    r = run_bass_kernel_spmd(nc, [arrays], core_ids=[0])
    return r.results[0]["out_0"].reshape(B, T, C)
```
